# Optimizing a Trainium2 kernel written in Bass

```python
import numpy as np
import jax
import jax.numpy as jnp

def _softmax(x, axis=-1):
    return jax.nn.softmax(x, axis=axis)

def _gelu(x):
    return jax.nn.gelu(x, approximate=True)

def _silu(x):
    return jax.nn.silu(x)

def _sigmoid(x):
    return jax.nn.sigmoid(x)

def _layernorm(x, axis=-1, eps=1e-05):
    m = jnp.mean(x, axis=axis, keepdims=True)
    v = jnp.var(x, axis=axis, keepdims=True)
    return (x - m) / jnp.sqrt(v + eps)

def _scatter_add(tgt, idx, src, axis=0):
    return tgt.at[idx].add(src)

def _segment_sum(src, seg, n):
    return jax.ops.segment_sum(src, seg, n)
kernel_name = 'mk_decoder_preln_d1_seqx_r4_0d55a5'

def setup_inputs(seed: int=0):
    np.random.seed(seed)
    _w = jnp.asarray

    def _rec_inputs():
        import jax
        import jax.numpy as jnp
        _rk = jax.random.key(seed)
        x = 0.0002417 + 0.9998 * jax.random.normal(jax.random.fold_in(_rk, 1), (4, 1024, 256), jnp.float32)
        _lenS = 1024 - jax.random.randint(jax.random.fold_in(_rk, 7), (4,), 0, max(1, 1024 // 4) + 1, jnp.int32)
        _lenS2 = 64 - jax.random.randint(jax.random.fold_in(_rk, 8), (4,), 0, max(1, 64 // 4) + 1, jnp.int32)
        _ctx_1024P = jax.random.normal(jax.random.fold_in(_rk, 11), (4, 16, 256), jnp.float32)
        _ctx_1024c = jax.random.dirichlet(jax.random.fold_in(_rk, 511), 0.3 * jnp.ones((16,), jnp.float32), (4, 64))
        _ctx_1024t = jnp.einsum('bsk,bkd->bsd', _ctx_1024c, _ctx_1024P)
        _ctx_1024t = _ctx_1024t * jax.lax.rsqrt(jnp.mean(jnp.square(_ctx_1024t)) + 1e-12) * 0.953939
        ctx_1024 = 7.22013e-05 + 1.00017 * (_ctx_1024t + 0.3 * jax.random.normal(jax.random.fold_in(_rk, 611), (4, 64, 256), jnp.float32))
        return (x, ctx_1024)
    x, ctx_1024 = _rec_inputs()

    def _L0_attn_setup():
        import jax, jax.numpy as jnp
        import numpy as np
        BSZ, T, DM, N = (8, 1024, 256, 64)
        LN_EPS = 1e-05
        key = jax.random.key(seed)
        ks = jax.random.split(key, 7)
        return {'x': jax.random.normal(ks[0], (BSZ, T, DM), jnp.float32), 'log_A': jax.random.normal(ks[1], (DM, N), jnp.float32) * 0.01 - 4.0, 'B_param': jax.random.normal(ks[2], (DM, N), jnp.float32) * 0.01, 'C_param': jax.random.normal(ks[3], (DM, N), jnp.float32) * 0.01, 'D_param': jnp.ones((DM,), jnp.float32), 'log_dt': jax.random.normal(ks[4], (DM,), jnp.float32) * 0.01 - 4.0, 'ln_gamma': jnp.ones((DM,), jnp.float32), 'ln_beta': jnp.zeros((DM,), jnp.float32), 'W_out': jax.random.normal(ks[5], (DM, DM), jnp.float32) / np.sqrt(DM).astype(np.float32), 'b_out': jnp.zeros((DM,), jnp.float32)}
    _L0_attn_all = _L0_attn_setup()
    _L0_attn_in = {k: v for k, v in _L0_attn_all.items() if k in ('log_A', 'B_param', 'C_param', 'D_param', 'log_dt', 'ln_gamma', 'ln_beta', 'W_out', 'b_out')}
    del _L0_attn_all

    def _L0_xattn_setup():
        import jax, jax.numpy as jnp
        import numpy as np
        N, S, E, H = (4, 512, 256, 16)
        D = E // H
        key = jax.random.key(seed)
        k1, k2, k3, k4 = jax.random.split(key, 4)
        return {'values': jax.random.normal(k1, (N, S, E), dtype=jnp.float32), 'keys': jax.random.normal(k2, (N, S, E), dtype=jnp.float32), 'query': jax.random.normal(k3, (N, S, E), dtype=jnp.float32), 'W_out': jax.random.normal(k4, (E, E), dtype=jnp.float32) * (1.0 / np.sqrt(E)), 'b_out': jnp.zeros((E,), dtype=jnp.float32)}
    _L0_xattn_all = _L0_xattn_setup()
    _L0_xattn_in = {k: v for k, v in _L0_xattn_all.items() if k in ('W_out', 'b_out')}
    del _L0_xattn_all

    def _L0_ffn_setup():
        import jax, jax.numpy as jnp
        import numpy as np
        D_IN, D_HID = (256, 1024)

        def _ternary(key, shape):
            return jax.random.randint(key, shape, -1, 2).astype(jnp.float32)

        def _tlin(x, w, s):
            return jnp.einsum('bsi,oi->bso', x, w) * s
        key = jax.random.key(seed)
        ks = jax.random.split(key, 12)
        inv = lambda fan: 1.0 / np.sqrt(fan).astype(np.float32)
        return {'x': jax.random.normal(ks[0], (4, 512, D_IN), dtype=jnp.float32), 'w1_w': _ternary(ks[1], (D_HID, D_IN)), 'w1_s': jax.random.uniform(ks[2], (D_HID,), dtype=jnp.float32) * inv(D_IN), 'w2_w': _ternary(ks[3], (D_HID, D_IN)), 'w2_s': jax.random.uniform(ks[4], (D_HID,), dtype=jnp.float32) * inv(D_IN), 'h1_w': _ternary(ks[5], (D_HID, D_HID)), 'h1_s': jax.random.uniform(ks[6], (D_HID,), dtype=jnp.float32) * inv(D_HID), 'h2_w': _ternary(ks[7], (D_HID, D_HID)), 'h2_s': jax.random.uniform(ks[8], (D_HID,), dtype=jnp.float32) * inv(D_HID), 'w3_w': _ternary(ks[9], (D_IN, D_HID)), 'w3_s': jax.random.uniform(ks[10], (D_IN,), dtype=jnp.float32) * inv(D_HID)}
    _L0_ffn_all = _L0_ffn_setup()
    _L0_ffn_in = {k: v for k, v in _L0_ffn_all.items() if k in ('w1_w', 'w1_s', 'w2_w', 'w2_s', 'h1_w', 'h1_s', 'h2_w', 'h2_s', 'w3_w', 'w3_s')}
    del _L0_ffn_all
    return {'x': x, 'ctx_1024': ctx_1024, 'L0_attn_log_A': _L0_attn_in['log_A'], 'L0_attn_B_param': _L0_attn_in['B_param'], 'L0_attn_C_param': _L0_attn_in['C_param'], 'L0_attn_D_param': _L0_attn_in['D_param'], 'L0_attn_log_dt': _L0_attn_in['log_dt'], 'L0_attn_ln_gamma': _L0_attn_in['ln_gamma'], 'L0_attn_ln_beta': _L0_attn_in['ln_beta'], 'L0_attn_W_out': _L0_attn_in['W_out'], 'L0_attn_b_out': _L0_attn_in['b_out'], 'L0_xattn_W_out': _L0_xattn_in['W_out'], 'L0_xattn_b_out': _L0_xattn_in['b_out'], 'L0_ffn_w1_w': _L0_ffn_in['w1_w'], 'L0_ffn_w1_s': _L0_ffn_in['w1_s'], 'L0_ffn_w2_w': _L0_ffn_in['w2_w'], 'L0_ffn_w2_s': _L0_ffn_in['w2_s'], 'L0_ffn_h1_w': _L0_ffn_in['h1_w'], 'L0_ffn_h1_s': _L0_ffn_in['h1_s'], 'L0_ffn_h2_w': _L0_ffn_in['h2_w'], 'L0_ffn_h2_s': _L0_ffn_in['h2_s'], 'L0_ffn_w3_w': _L0_ffn_in['w3_w'], 'L0_ffn_w3_s': _L0_ffn_in['w3_s']}

def reference(x, ctx_1024, L0_attn_log_A, L0_attn_B_param, L0_attn_C_param, L0_attn_D_param, L0_attn_log_dt, L0_attn_ln_gamma, L0_attn_ln_beta, L0_attn_W_out, L0_attn_b_out, L0_xattn_W_out, L0_xattn_b_out, L0_ffn_w1_w, L0_ffn_w1_s, L0_ffn_w2_w, L0_ffn_w2_s, L0_ffn_h1_w, L0_ffn_h1_s, L0_ffn_h2_w, L0_ffn_h2_s, L0_ffn_w3_w, L0_ffn_w3_s):
    import jax
    import jax.numpy as jnp

    def _L0_attn_ref(x, log_A, B_param, C_param, D_param, log_dt, ln_gamma, ln_beta, W_out, b_out):
        import jax, jax.numpy as jnp
        import numpy as np
        BSZ, T, DM, N = (8, 1024, 256, 64)
        LN_EPS = 1e-05
        residual = x
        mu = jnp.mean(x, axis=-1, keepdims=True)
        var = jnp.mean(jnp.square(x - mu), axis=-1, keepdims=True)
        xn = (x - mu) / jnp.sqrt(var + LN_EPS) * ln_gamma + ln_beta
        dt = jnp.exp(log_dt)
        dA = jnp.exp(-jnp.exp(log_A) * dt[:, None])
        dB = B_param * dt[:, None]

        def step(h, u):
            h = dA * h + dB * u[..., None]
            y = jnp.einsum('dn,bdn->bd', C_param, h) + D_param * u
            return (h, y)
        h0 = jnp.zeros((x.shape[0], x.shape[2], dA.shape[1]), x.dtype)
        _, ys = jax.lax.scan(step, h0, jnp.swapaxes(xn, 0, 1))
        y = jnp.swapaxes(ys, 0, 1)
        y = jnp.einsum('btd,ed->bte', y, W_out) + b_out
        return residual + y

    def _L0_xattn_ref(values, keys, query, W_out, b_out):
        import jax, jax.numpy as jnp
        import numpy as np
        N, S, E, H = (4, 512, 256, 16)
        D = E // H
        n = query.shape[0]
        v = values.reshape(n, -1, H, D)
        k = keys.reshape(n, -1, H, D)
        q = query.reshape(n, -1, H, D)
        energy = jnp.einsum('nqhd,nkhd->nhqk', q, k)
        attn = jax.nn.softmax(energy / jnp.sqrt(jnp.float32(D)), axis=-1)
        out = jnp.einsum('nhqk,nkhd->nqhd', attn, v).reshape(n, -1, E)
        return out @ W_out.T + b_out

    def _L0_ffn_ref(x, w1_w, w1_s, w2_w, w2_s, h1_w, h1_s, h2_w, h2_s, w3_w, w3_s):
        import jax, jax.numpy as jnp
        import numpy as np
        D_IN, D_HID = (256, 1024)

        def _ternary(key, shape):
            return jax.random.randint(key, shape, -1, 2).astype(jnp.float32)

        def _tlin(x, w, s):
            return jnp.einsum('bsi,oi->bso', x, w) * s
        h = jax.nn.silu(_tlin(x, w1_w, w1_s)) * _tlin(x, w2_w, w2_s)
        h = jax.nn.gelu(_tlin(h, h1_w, h1_s), approximate=False)
        h = jax.nn.gelu(_tlin(h, h2_w, h2_s), approximate=False)
        return _tlin(h, w3_w, w3_s)
    x = x + _L0_attn_ref(_layernorm(x, axis=-1), L0_attn_log_A, L0_attn_B_param, L0_attn_C_param, L0_attn_D_param, L0_attn_log_dt, L0_attn_ln_gamma, L0_attn_ln_beta, L0_attn_W_out, L0_attn_b_out)
    x = x + _L0_xattn_ref(ctx_1024, ctx_1024, _layernorm(x, axis=-1), L0_xattn_W_out, L0_xattn_b_out)
    x = x + _L0_ffn_ref(_layernorm(x, axis=-1), L0_ffn_w1_w, L0_ffn_w1_s, L0_ffn_w2_w, L0_ffn_w2_s, L0_ffn_h1_w, L0_ffn_h1_s, L0_ffn_h2_w, L0_ffn_h2_s, L0_ffn_w3_w, L0_ffn_w3_s)
    return x

_drawn_inputs = setup_inputs


def setup_inputs(seed=0):
    import zlib

    import numpy as np

    out = dict(_drawn_inputs(seed))
    spreads = {'L0_attn_D_param': (1.0, 0.2),
     'L0_attn_ln_gamma': (1.0, 0.2),
     'L0_attn_ln_beta': (0.0, 0.1),
     'L0_attn_b_out': (0.0, 0.1),
     'L0_xattn_b_out': (0.0, 0.1)}
    factors = {}
    for name, (base, spread) in spreads.items():
        noise = np.random.default_rng([zlib.crc32(name.encode()), seed]).standard_normal(out[name].shape)
        drawn = base * np.exp(spread * noise) if base else spread * noise
        out[name] = jnp.asarray(drawn.astype(out[name].dtype))
    for name, factor in factors.items():
        out[name] = (out[name] * factor).astype(out[name].dtype)
    return out
```

```python
import numpy as np
import concourse.bass as bass
from concourse import mybir
from contextlib import ExitStack

F32 = mybir.dt.float32
F32R = mybir.dt.float32r
I32 = mybir.dt.int32
ACT = mybir.ActivationFunctionType
ALU = mybir.AluOpType
AX = mybir.AxisListType

P = 128
BATCH, T, DM = 4, 1024, 256
N = 64
L = 64
CH = T // L
BC = BATCH * CH
TOK = BATCH * T
TILES = TOK // P
KEYS, HEADS, HD = 64, 16, 16
HID = 1024
BLK = 512
NBLK = TOK // BLK
TPB = BLK // P
EPS = 1e-5
DH = DM // P
HC = HID // P
OCT = 8
GRP = 16
NGRP = DM // GRP


def mixer_program(nc, ctx, a, t):
    def sb(name, shape, dt=F32):
        return ctx.enter_context(nc.sbuf_tensor(name, shape, dt))

    def sem(name):
        return ctx.enter_context(nc.semaphore(name))

    V = sb("V", [P, DM, BC])
    Vf = V[:, :, :].rearrange("p d c -> p (d c)")
    V4 = V[:, :, :].rearrange("p d (b c) -> p d b c", b=BATCH)
    xres = sb("xres", [P, TILES, DM])
    ring = sb("ring", [P, 4096])
    dec = sb("dec", [P, 2, OCT * BC])
    zt = dec[:, :, :].rearrange("p a (b m) -> p (a b) m", b=2)
    stage = sb("stage", [P, 2, 1024])
    gam = sb("gam", [P, DM])
    bet = sb("bet", [P, DM])
    bo = sb("bo", [P, DM])
    a64 = sb("a64", [N, DM])
    woT = sb("woT", [P, DH, DM])
    rev = sb("rev", [P, P])
    ones = sb("ones", [P, 32])
    esc = sb("esc", [L, 1])
    st = sb("st", [P, 4, 6])
    mv4 = sb("mv4", [P, 4, 2])
    mv = sb("mv", [P, TILES, 2])
    small = sb("small", [P, 6, TILES])
    ve, r1, v2, r2, rr, nm = (small[:, k, :] for k in range(6))
    nmr = sb("nmr", [P, TILES])
    mhalf = sb("mhalf", [P, TILES])
    dtc = sb("dtc", [P, 4])
    pk = ring[:, 0:6 * DM].rearrange("p (k d) -> p k d", k=6)
    ksb = ring[:, 2048:3072].rearrange("p (a m) -> p a m", a=2)
    dbc = ring[:, 1536:1600].rearrange("p (u c) -> p u c", u=8)
    natA = ring[:, 3072:3200].rearrange("p (h n) -> p h n", h=DH)
    natB = ring[:, 3200:3328].rearrange("p (h n) -> p h n", h=DH)
    natC = ring[:, 3328:3456].rearrange("p (h n) -> p h n", h=DH)
    al2 = ring[:, 3456:3712].rearrange("p (h u n) -> p h u n", h=DH, u=2)
    w2d = ring[:, 3712:3968].rearrange("p (h u n) -> p h u n", h=DH, u=2)
    TG = [ring[:, 1024 * k:1024 * (k + 1)] for k in range(2)]
    EE = [ring[:, 1024 * (2 + k):1024 * (3 + k)] for k in range(2)]
    yT = [ring[:, 1024 * k:1024 * (k + 1)] for k in range(2)]
    zb = [ring[:, 1024 * (2 + k):1024 * (3 + k)] for k in range(2)]
    pair = t["pair"]
    coefT = pair[3][:, 0:512]
    alT = pair[3][:, 0:DM]
    wT = pair[3][:, 512:512 + DM]
    hps = [pair[1][:, 512 * k:512 * (k + 1)] for k in range(2)]
    yps = [pair[2][:, 512 * k:512 * (k + 1)] for k in range(2)]
    kps = [pair[3][:, 512 * k:512 * (k + 1)] for k in range(2)]
    wps = [pair[0], pair[2]]
    ident = t["ident"]
    kr, alS, x1d = t["kr"], t["alS"], t["x1d"]

    coef_in, bc_in, x_in, d_in, scl_in = (sem(n) for n in ("coef_in", "bc_in", "x_in", "d_in", "scl_in"))
    const, exps, coef, al_st = sem("const"), sem("exps"), sem("coef"), sem("al_st")
    coef_t, pk_done, g_row, k_ps, k_ev, k_d = (sem(n) for n in ("coef_t", "pk_done", "g_row", "k_ps", "k_ev", "k_d"))
    kr_st = [sem("kr_st0"), sem("kr_st1")]
    kr_pad = sem("kr_pad")
    mv_cp, stat, aggr, lnm, powd, z_rdy, z_g, zt_free = (sem(n) for n in ("mv_cp", "stat", "aggr", "lnm", "powd", "z_rdy", "z_g", "zt_free"))
    w_in = [sem("w_in0"), sem("w_in1")]
    w_t, w_ev = sem("w_t"), sem("w_ev")
    A_in, T_in = [sem("A_in0"), sem("A_in1")], [sem("T_in0"), sem("T_in1")]
    t_mask, e_rdy, g_cp, h_ps, h_scan, dec_rdy = (sem(n) for n in ("t_mask", "e_rdy", "g_cp", "h_ps", "h_scan", "dec_rdy"))
    y_ps, y_out, dec0, ezero = sem("y_ps"), sem("y_out"), sem("dec0"), sem("ezero")
    y_t, y_tev, pr_ps, zb_rdy, zb_b, x1a, x1_rdy = (sem(n) for n in ("y_t", "y_tev", "pr_ps", "zb_rdy", "zb_b", "x1a", "x1_rdy"))
    x1_st = [sem("x1_st0"), sem("x1_st1")]
    step_v, step_t, step_g = (sem(n) for n in ("step_v", "step_t", "step_g"))

    w1v = a["w1"].rearrange("(u c p) k -> u p c k", c=4, p=P)
    h1v = a["h1"].rearrange("(u p) k -> u p k", p=P)
    h2v = a["h2"].rearrange("(u p) k -> u p k", p=P)
    awv = a["aW"].rearrange("(c p) k -> p c k", p=P)
    xv = a["x"].rearrange("b t d -> (b t) d").rearrange("(k j p) d -> k p j d", j=4, p=P)
    x1v = x1d.rearrange("(k j p) d -> k p j d", j=4, p=P)
    NW = 3 + 2 * HC

    def tg_load(e, g, p):
        e.dma_start(TG[p][0:L, :], bass.AP(t["kr_h"], g * (GRP * L), [[1, L], [1, GRP * L]])).then_inc(T_in[p], 16)

    def al_load(e, g, p):
        e.dma_start(EE[p][0:L, :], bass.AP(t["alS_h"], g * (GRP * N), [[0, L], [1, GRP * N]])).then_inc(A_in[p], 16)

    block = ctx.enter_context(nc.Block())

    @block.sync
    def _(e):
        for v, dst in ((a["logA"], natA), (a["Bp"], natB), (a["Cp"], natC)):
            e.dma_start(dst, v.rearrange("(h p) n -> p h n", p=P)).then_inc(coef_in, 16)
        for h in range(DH):
            e.dma_start(dtc[:, h:h + 1], a["log_dt"][h * P:(h + 1) * P].rearrange("(p o) -> p o", o=1)).then_inc(coef_in, 16)
        for k in range(TILES // 4):
            e.dma_start(xres[:, 4 * k:4 * k + 4, :], xv[k]).then_inc(x_in, 16)
        for v, dst in ((a["gamma"], gam), (a["beta"], bet), (a["ab"], bo)):
            e.dma_start(dst[:, :], v.partition_broadcast(P)).then_inc(bc_in, 16)
        dq = a["Dp"].rearrange("(u q c) -> q u c", u=8, q=4)
        for q in range(4):
            e.dma_start(dbc[32 * q:32 * q + 32, :, :], dq[q].partition_broadcast(32)).then_inc(d_in, 16)
        for v, c0, n in ((a["s1"], 0, HC), (a["s2"], HC, HC), (a["hs1"], 2 * HC, HC), (a["hs2"], 3 * HC, HC), (a["s3"], 4 * HC, DH)):
            for c in range(n):
                e.dma_start(t["scl"][:, c0 + c:c0 + c + 1], v[c * P:(c + 1) * P].rearrange("(p o) -> p o", o=1)).then_inc(scl_in, 16)
        e.wait_ge(coef, 4)
        e.dma_start(alS.rearrange("(h p) n -> p h n", p=P), al2[:, :, 0, :]).then_inc(al_st, 16)
        for u in range(2):
            e.dma_start(stage[:, u, :].rearrange("p (c k) -> p c k", c=4), w1v[u]).then_inc(w_in[u], 16)
        e.wait_ge(w_t, 1)
        e.dma_start(stage[:, 0, 0:512].rearrange("p (c k) -> p c k", c=2), awv).then_inc(w_in[0], 16)
        for v, base in ((h1v, 0), (h2v, HC)):
            with e.Fori(0, HC // 2) as k:
                for q in range(2):
                    e.wait_ge(w_t, 2 * k + (base + q + 2))
                    e.dma_start(stage[:, 1 - q, :], v[bass.ds(2 * k + q, 1)].rearrange("a p k -> (a p) k")).then_inc(w_in[1 - q], 16)
        e.wait_ge(al_st, 16)
        for s in kr_st:
            e.wait_ge(s, 64)
        e.wait_ge(kr_pad, 16)
        for g in range(2):
            al_load(e, g, g)
            tg_load(e, g, g)
        with e.Fori(1, NGRP // 2) as it:
            for p in range(2):
                e.wait_ge(h_ps, 4 * it + (2 * p - 2))
                al_load(e, 2 * it + p, p)
                e.wait_ge(y_ps, 4 * it + (2 * p - 2))
                tg_load(e, 2 * it + p, p)
        with e.Fori(0, NBLK // 2) as it:
            for p in range(2):
                e.wait_ge(x1_rdy, 2 * it + (p + 2))
                e.dma_start(x1v[bass.ds(2 * it + p, 1)].rearrange("a p j d -> (a p) j d"),
                            xres[:, bass.ds(8 * it + 4 * p, 4), :]).then_inc(x1_st[p], 16)
        for s in x1_st:
            e.wait_ge(s, 16 * NBLK // 2)
        e.wait_ge(scl_in, 16 * (4 * HC + DH))

    @block.gpsimd
    def _(e):
        e.memset(ident[:, :], 0.0).then_inc(const, 1)
        e.memset(rev[:, :], 0.0).then_inc(const, 1)
        e.memset(ones[:, :], 1.0).then_inc(const, 1)
        e.memset(mhalf[:, :], -0.5).then_inc(const, 1)
        e.iota(esc[:, :], [[0, 1]], base=-L, channel_multiplier=1, allow_small_or_imprecise_dtypes=True).then_inc(const, 1)
        e.wait_ge(const, 5)
        e.affine_select(out=ident[:, :], in_=ident[:, :], compare_op=ALU.not_equal, fill=1.0, base=0,
                        pattern=[[-1, P]], channel_multiplier=1).then_inc(const, 1)
        for h in range(2):
            blk = rev[64 * h:64 * h + 64, 64 * h:64 * h + 64]
            e.wait_ge(const, 6 + h)
            e.affine_select(out=blk, in_=blk, compare_op=ALU.not_equal, fill=1.0, base=-63,
                            pattern=[[1, 64]], channel_multiplier=1).then_inc(const, 1)
        e.wait_ge(const, 8)
        e.dma_start(kr[:, DM * L:DM * L + L], rev[0:1, L:2 * L]).then_inc(kr_pad, 16)
        for u in range(8):
            e.wait_ge(k_d, u + 1)
            e.dma_start(kr[0, u * 2048:(u + 1) * 2048].rearrange("(q m) -> q m", q=4), ksb[0:P:32, u % 2, :]).then_inc(kr_st[u % 2], 16)
        e.wait_ge(lnm, 1)
        e.tensor_tensor(r1, ve, mhalf[:, :], ALU.pow).then_inc(powd, 1)
        e.wait_ge(lnm, 4)
        e.tensor_tensor(r2, v2, mhalf[:, :], ALU.pow).then_inc(powd, 1)
        e.wait_ge(bc_in, 48)
        with e.Fori(0, TILES // 4) as k:
            for j in range(4):
                e.wait_ge(z_rdy, 4 * k + (j + 1))
                e.tensor_tensor(zt[:, j, :], zt[:, j, :], gam[:, :], ALU.mult).then_inc(z_g, 1)
        for s in kr_st:
            e.wait_ge(s, 64)
        e.wait_ge(z_g, TILES)
        for p in range(2):
            e.memset(EE[p][N:P, :], 0.0).then_inc(ezero, 1)
        e.wait_ge(ezero, 2)

        def mask(g, p, turn):
            e.wait_ge(T_in[p], 16 * turn)
            e.sem_inc(step_g, 1)
            v = TG[p][0:L, :].rearrange("p (d t) -> p d t", d=GRP)
            e.affine_select(out=v, in_=v, compare_op=ALU.is_ge, fill=0.0, base=L - 1,
                            pattern=[[0, GRP], [-1, L]], channel_multiplier=-1).then_inc(t_mask, 1)
        with e.Fori(0, NGRP // 2) as it:
            for p in range(2):
                mask(2 * it + p, p, it + 1)
        with e.Fori(0, NBLK // 2) as it:
            for p in range(2):
                e.wait_ge(zb_rdy, 8 * it + 4 * (p + 1))
                for j in range(4):
                    v = zb[p][:, j * DM:(j + 1) * DM]
                    e.tensor_tensor(v, v, bo[:, :], ALU.add).then_inc(zb_b, 1)

    @block.scalar
    def _(e):
        e.wait_ge(coef_in, 80)
        e.activation(dtc[:, 2:4], dtc[:, 0:2], ACT.Exp).then_inc(exps, 1)
        e.activation(natA, natA, ACT.Exp).then_inc(exps, 1)
        e.wait_ge(coef_t, 1)
        e.activation(a64[:, :], alT[0:N, :], ACT.Exp, scale=-float(L)).then_inc(pk_done, 1)
        for k in range(6):
            e.activation(pk[N:P, k, :], alT[N:P, :], ACT.Exp, scale=-float(2 ** k)).then_inc(pk_done, 1)
        for u in range(8):
            e.wait_ge(k_ps, u + 1)
            if u >= 2:
                e.wait_ge(kr_st[u % 2], 16 * (u // 2))
            e.activation(ksb[:, u % 2, :], kps[u % 2], ACT.Copy).then_inc(k_ev, 1)

        def w_evac(u, dst, src):
            e.wait_ge(w_t, u + 1)
            e.activation(dst, src, ACT.Copy).then_inc(w_ev, 1)
        for u in range(2):
            w_evac(u, t["w1T"][:, :, 512 * u:512 * u + 512].rearrange("p k (c o) -> p c k o", c=4),
                   wps[u][:, :].rearrange("p (c k o) -> p c k o", c=4, k=DH))
        w_evac(2, woT[:, :, :].rearrange("p k (c o) -> p c k o", c=2), wps[0][:, 0:512].rearrange("p (c k o) -> p c k o", c=2, k=DH))
        e.wait_ge(lnm, 7)
        for name, base in (("h1T", 0), ("h2T", HC)):
            with e.Fori(0, HC // 2) as k:
                for q in range(2):
                    w_evac(3 + base + 2 * k + q, t[name][:, :, bass.ds(2 * P * k + P * q, P)],
                           wps[1 - q][:, :].rearrange("p (k o) -> p k o", k=HC))
                for j in range(4):
                    tile = 4 * k + (4 * base // 2 + j)
                    e.wait_ge(zt_free, tile + 1)
                    e.activation(zt[:, j, :].unsqueeze(1), xres[:, bass.ds(tile, 1), :], ACT.Identity,
                                 bias=nm[:, bass.ds(tile, 1)], scale=rr[:, bass.ds(tile, 1)]).then_inc(z_rdy, 1)
        e.wait_ge(const, 8)

        def prep(g, p, turn):
            e.wait_ge(A_in[p], 16 * turn)
            e.activation(EE[p][0:L, :], EE[p][0:L, :], ACT.Exp, scale=esc[:, :]).then_inc(e_rdy, 1)
            e.activation(TG[p][N:P, :], Vf[N:P, bass.ds(g * (GRP * L), GRP * L)], ACT.Copy).then_inc(g_cp, 1)

        def turns(it, half, last):
            for q in range(4):
                o = 4 * it + q
                e.wait_ge(y_ps, o + 1)
                e.activation(Vf[64 * half:64 * half + 64, bass.ds(o * 512 - half * (P * BC), 512)], yps[q % 2][0:L, :], ACT.Copy).then_inc(y_out, 1)
                if q % 2 == 1 and not last:
                    prep(2 * it + (2 + q // 2), q // 2, it + 2)
        e.wait_ge(kr_st[0], 64)
        e.wait_ge(kr_st[1], 64)
        prep(0, 0, 1)
        prep(1, 1, 1)
        half_turns = NGRP // 4
        with e.Fori(0, half_turns) as it:
            turns(it, 0, False)
        with e.Fori(half_turns, 2 * half_turns - 1) as it:
            turns(it, 1, False)
        turns(2 * half_turns - 1, 1, True)
        with e.Fori(0, NBLK // 2) as it:
            for p in range(2):
                for j in range(4):
                    tile = 8 * it + (4 * p + j)
                    if j == 0:
                        e.wait_ge(x1_rdy, 2 * it + p)
                    e.activation(zb[p][:, j * DM:(j + 1) * DM].unsqueeze(1), xres[:, bass.ds(tile, 1), :], ACT.Identity,
                                 bias=nmr[:, bass.ds(tile, 1)], scale=r1[:, bass.ds(tile, 1)]).then_inc(zb_rdy, 1)
                e.wait_ge(y_t, 2 * it + (p + 1))
                e.activation(yT[p].rearrange("p (h c t) -> p c h t", h=DH, c=8),
                             pair[p][:, :].rearrange("p (c h t) -> p c h t", c=8, h=DH), ACT.Copy).then_inc(y_tev, 1)

    @block.vector
    def _(e):
        e.wait_ge(exps, 2)
        for h in range(DH):
            for d in range(2):
                e.tensor_scalar(al2[:, h, d, :], natA[:, h, :], dtc[:, 2 + h:3 + h], None, ALU.mult).then_inc(coef, 1)
        e.tensor_tensor(natB, natB, natC, ALU.mult).then_inc(coef, 1)
        e.wait_ge(coef, 5)
        for h in range(DH):
            for d in range(2):
                e.tensor_scalar(w2d[:, h, d, :], natB[:, h, :], dtc[:, 2 + h:3 + h], None, ALU.mult).then_inc(coef, 1)
        e.wait_ge(coef_t, 1)
        e.tensor_copy(V[N:P, :, L - 1:L], wT[N:P, :].unsqueeze(2)).then_inc(g_row, 1)
        for k in range(6):
            n = 2 ** k
            e.wait_ge(pk_done, k + 2)
            e.wait_ge(g_row, k + 1)
            e.tensor_tensor(V[N:P, :, L - 2 * n:L - n], V[N:P, :, L - n:L],
                            pk[N:P, k, :].unsqueeze(2).to_broadcast([N, DM, n]), ALU.mult).then_inc(g_row, 1)
        e.wait_ge(x_in, 16 * TILES // 4)
        with e.Fori(0, TILES // 4) as k:
            e.wait_ge(aggr, 4 * k)
            for j in range(4):
                e.bn_stats(st[:, j, :], xres[:, bass.ds(4 * k + j, 1), :].rearrange("p a d -> p (a d)")).then_inc(stat, 1)
            e.wait_ge(stat, 4 * k + 4)
            e.wait_ge(mv_cp, k)
            e.sem_inc(step_v, 1)
            for j in range(4):
                e.bn_aggr(mv4[:, j, :], st[:, j, :]).then_inc(aggr, 1)
            e.wait_ge(aggr, 4 * k + 4)
            e.tensor_copy(mv[:, bass.ds(4 * k, 4), :], mv4[:, :, :]).then_inc(mv_cp, 1)
        e.wait_ge(d_in, 64)
        for u in range(8):
            e.wait_ge(k_ev, u + 1)
            v = ksb[:, u % 2, :].rearrange("p (c t) -> p c t", c=8)[:, :, L - 1]
            e.tensor_tensor(v, v, dbc[:, u, :], ALU.add).then_inc(k_d, 1)
        e.wait_ge(mv_cp, TILES // 4)
        mean, var = mv[:, :, 0], mv[:, :, 1]
        e.tensor_scalar_add(ve, var, EPS).then_inc(lnm, 1)
        e.wait_ge(powd, 1)
        e.tensor_tensor(v2, r1, r1, ALU.mult).then_inc(lnm, 1)
        e.wait_ge(lnm, 2)
        e.tensor_tensor(v2, v2, var, ALU.mult).then_inc(lnm, 1)
        e.wait_ge(lnm, 3)
        e.tensor_scalar_add(v2, v2, EPS).then_inc(lnm, 1)
        e.wait_ge(powd, 2)
        e.tensor_tensor(rr, r1, r2, ALU.mult).then_inc(lnm, 1)
        e.wait_ge(lnm, 5)
        e.scalar_tensor_tensor(nm, mean, -1.0, rr, ALU.mult, ALU.mult).then_inc(lnm, 1)
        e.scalar_tensor_tensor(nmr[:, :], mean, -1.0, r1, ALU.mult, ALU.mult).then_inc(lnm, 1)
        e.memset(zt[:, 0, 0:1], 0.0).then_inc(zt_free, 4)
        e.wait_ge(bc_in, 48)
        e.wait_ge(zt_free, 4)
        with e.Fori(0, TILES // 4) as k:
            for j in range(4):
                tile = 4 * k + j
                e.wait_ge(z_g, tile + 1)
                e.tensor_tensor(V[0:L, :, bass.ds(8 * k + 2 * j, 1)], zt[0:64, j, :].unsqueeze(2), bet[0:64, :].unsqueeze(2), ALU.add)
                e.tensor_tensor(V[0:L, :, bass.ds(8 * k + (2 * j + 1), 1)], zt[64:P, j, :].unsqueeze(2), bet[64:P, :].unsqueeze(2), ALU.add).then_inc(zt_free, 1)
        e.wait_ge(zt_free, TILES + 4)
        for k in range(2):
            e.memset(dec[0:N, k, :], 0.0).then_inc(dec0, 1)
        for k in range(2):
            e.memset(hps[k][0:N, :], 0.0).then_inc(h_scan, 1)
        e.wait_ge(dec0, 2)
        e.memset(dec[N:P, 0, 0:1], 0.0).then_inc(x1_rdy, 1)
        with e.Fori(0, DM // OCT // 4) as it:
            for q in range(4):
                o = 4 * it + q
                dv = dec[0:N, q % 2, :].rearrange("p (d b c) -> p d b c", d=OCT, b=BATCH)[:, :, :, 1:CH]
                e.wait_ge(h_scan, o + 1)
                e.tensor_copy(dv, a64[:, bass.ds(OCT * 4 * it + OCT * q, OCT)].unsqueeze(2).unsqueeze(3).to_broadcast([N, OCT, BATCH, CH - 1])).then_inc(dec_rdy, 1)
                e.wait_ge(dec_rdy, o + 1)
                e.wait_ge(h_ps, o + 1)
                if q % 2 == 0:
                    e.wait_ge(g_cp, 2 * it + (q // 2 + 1))
                e.tensor_tensor_scan(Vf[N:P, bass.ds(2048 * it + 512 * q, 512)], dec[0:N, q % 2, :], hps[q % 2][0:N, :], 0.0,
                                     ALU.mult, ALU.add).then_inc(h_scan, 1)
        with e.Fori(0, NBLK // 2) as it:
            for p in range(2):
                e.wait_ge(zb_b, 8 * it + 4 * (p + 1))
                e.wait_ge(pr_ps, 2 * it + (p + 1))
                e.tensor_tensor(zb[p], pair[2 + p][:, :], zb[p], ALU.add).then_inc(x1a, 1)
                e.wait_ge(x1a, 2 * it + (p + 1))
                v = xres[:, bass.ds(8 * it + 4 * p, 4), :].rearrange("p j d -> p (j d)")
                e.tensor_tensor(v, v, zb[p], ALU.add).then_inc(x1_rdy, 1)

    @block.tensor
    def _(e):
        e.wait_ge(const, 8)
        e.wait_ge(coef, 9)
        for h in range(DH):
            e.transpose(alT[:, h * P:(h + 1) * P], al2[:, h, :, :].rearrange("p u n -> p (u n)"), ident[:, :])
        for h in range(DH):
            ins = e.transpose(wT[:, h * P:(h + 1) * P], w2d[:, h, :, :].rearrange("p u n -> p (u n)"), ident[:, :])
        ins.then_inc(coef_t, 1)
        e.wait_ge(g_row, 7)
        for u in range(8):
            if u >= 2:
                e.wait_ge(k_ev, u - 1)
            for q in range(4):
                c = u * 32 + q * 8
                ins = e.matmul(kps[u % 2][32 * q:32 * q + 32, :], ones[N:P, 0:32], Vf[N:P, c * L:(c + 8) * L], start=True, stop=True)
            ins.then_inc(k_ps, 1)

        def w_transposes(u, s, ps, srcs):
            for n, src in enumerate(srcs):
                ins = e.transpose(ps[:, n * P:(n + 1) * P], src, ident[:, :])
            ins.then_inc(w_t, 1)
        for u in range(3):
            e.wait_ge(w_in[u % 2], 16 * (u // 2 + 1))
            if u >= 2:
                e.wait_ge(w_ev, u - 1)
            w_transposes(u, u % 2, wps[u % 2], [stage[:, u % 2, n * P:(n + 1) * P] for n in range(8 if u < 2 else 4)])
        for base in (0, HC):
            with e.Fori(0, HC // 2) as k:
                for q in range(2):
                    e.wait_ge(w_in[1 - q], 16 * k + 16 * (base // 2 + 2 + q))
                    e.wait_ge(w_ev, 2 * k + (base + q + 2))
                    w_transposes(0, 1 - q, wps[1 - q], [stage[:, 1 - q, n * P:(n + 1) * P] for n in range(8)])
        e.wait_ge(zt_free, TILES + 4)
        e.wait_ge(ezero, 2)

        def states(o8, q, first_wait):
            e.wait_ge(*first_wait)
            for c in range(OCT):
                rhs = V4[:, bass.ds(o8 + c, 1), :, 0:CH - 1].rearrange("p a b c -> p (a b) c")
                out = hps[q % 2][0:N, c * BC:(c + 1) * BC].rearrange("p (b c) -> p b c", b=BATCH)[:, :, 1:CH]
                k = (q % 2) * OCT + c
                ins = e.matmul(out, EE[q // 2 % 2][:, k * N:(k + 1) * N], rhs, start=True, stop=True)
            ins.then_inc(h_ps, 1)

        def outputs(o8, q):
            e.sem_inc(step_t, 1)
            for c in range(OCT):
                k = (q % 2) * OCT + c
                rhs = V[:, bass.ds(o8 + c, 1), :].rearrange("p a c -> p (a c)")
                ins = e.matmul(yps[q % 2][0:L, c * BC:(c + 1) * BC], TG[q // 2][:, k * L:(k + 1) * L], rhs, start=True, stop=True)
            ins.then_inc(y_ps, 1)

        def turn(it, last):
            for q in range(4):
                if not (last and q == 3):
                    if q % 2 == 1:
                        e.wait_ge(e_rdy, 2 * it + ((q + 1) // 2 + 1))
                    states(32 * it + OCT * (q + 1), (q + 1) % 4, (h_scan, 4 * it + (q + 2)))
                if q % 2 == 0:
                    e.wait_ge(t_mask, 2 * it + (q // 2 + 1))
                    e.wait_ge(g_cp, 2 * it + (q // 2 + 1))
                e.wait_ge(h_scan, 4 * it + (q + 3))
                if not (isinstance(it, int) and 4 * it + q < 2):
                    e.wait_ge(y_out, 4 * it + (q - 1))
                outputs(32 * it + OCT * q, q)
        e.wait_ge(e_rdy, 1)
        states(0, 0, (h_scan, 1))
        turn(0, False)
        with e.Fori(1, DM // OCT // 4 - 1) as it:
            turn(it, False)
        turn(DM // OCT // 4 - 1, True)

        def y_transposes(i):
            if i >= 2:
                e.wait_ge(y_tev, i - 1)
            for c in range(8):
                ins = e.transpose(pair[i % 2][:, c * P:(c + 1) * P], V[:, 0:P, 8 * i + c], rev[:, :])
            ins.then_inc(y_t, 1)

        def project(i):
            e.wait_ge(y_tev, i + 1)
            if i >= 2:
                e.wait_ge(x1a, i - 1)
            for j in range(TPB):
                for h in range(DH):
                    ins = e.matmul(pair[2 + i % 2][:, j * DM:(j + 1) * DM], yT[i % 2][:, h * BLK + j * P:h * BLK + (j + 1) * P],
                                   woT[:, h, :], start=(h == 0), stop=(h == DH - 1))
            ins.then_inc(pr_ps, 1)
        e.wait_ge(w_ev, NW)
        e.wait_ge(y_out, DM // OCT)
        y_transposes(0)
        for i in range(NBLK):
            if i + 1 < NBLK:
                y_transposes(i + 1)
            project(i)


def attention_ffn_program(nc, ctx, a, t):
    def sb(name, shape, dt=F32):
        return ctx.enter_context(nc.sbuf_tensor(name, shape, dt))

    def sem(name):
        return ctx.enter_context(nc.semaphore(name))

    h1 = [sb("h1hi", [P, HC, BLK], F32R), sb("h1lo", [P, HC, BLK], F32R)]
    h2 = [sb("h2hi", [P, HC, BLK], F32R), sb("h2lo", [P, HC, BLK], F32R)]
    zT = [sb("zThi", [P, DH * BLK], F32R), sb("zTlo", [P, DH * BLK], F32R)]
    w2T = sb("w2T", [P, DH, HID], F32R)
    w3T = sb("w3T", [P, HC, DM], F32R)
    x1t = sb("x1t", [P, TPB * DM])
    xr = sb("xr", [P, TPB * DM])
    nat = sb("nat", [P, TPB, DM])
    qa = sb("qa", [P, DH, BLK])
    prob = sb("prob", [P, 2, BLK])
    pT = sb("pT", [P, 4, BLK])
    vb = sb("vbuf", [P, 2, BLK])
    sg = sb("sg", [P, 2, BLK])
    kblk = sb("kblk", [P, 2 * BLK])
    vblk = sb("vblk", [P, DM])
    xwoT = sb("xwoT", [P, DH, DM])
    xbo = sb("xbo", [P, DM])
    hmask = sb("hmask", [P, 8])
    st = sb("st2", [P, TPB, 6])
    mv = sb("mv2", [P, TPB, 2])
    lnv = sb("lnv", [P, 3, TPB])
    ve, rs, mh = lnv[:, 0, :], lnv[:, 1, :], lnv[:, 2, :]
    red = sb("red", [P, 3, 2, 8])
    bits = sb("bits", [P, BLK], I32)
    most = sb("most", [P, 1], I32)
    warm = sb("warm", [P, 2])
    bit_row = sb("bit_row", [1, P], I32)
    pair, ident, scl = t["pair"], t["ident"], t["scl"]
    x1d, x2d, kd, vd = t["x1d"], t["x2d"], t["kd"], t["vd"]
    w1T, h1T, h2T = t["w1T"], t["h1T"], t["h2T"]
    stage = [x1t, xr]
    c2 = pT[:, 0:2, :].rearrange("p a (b d) -> p (a b) d", d=DM)
    kst = [kblk[:, :], nat[:, :, :].rearrange("p j d -> p (j d)")]
    vst = qa[:, :, :].rearrange("p a (b d) -> p (a b) d", d=DM)
    t_ps = [pair[3][:, 512 * k:512 * (k + 1)] for k in range(2)]
    h_ps = [pair[k // 2][:, 512 * (k % 2):512 * (k % 2) + 512] for k in range(4)]
    sc1, sc2, sch, sc3 = scl[:, 0:8], scl[:, 8:16], (scl[:, 16:24], scl[:, 24:32]), scl[:, 32:34]

    w_in = [sem("pw_in0"), sem("pw_in1")]
    names = ("pw_t", "pw_ev", "c_in", "xbo_in", "mk", "pc_t", "kb_rdy", "vb_rdy", "vb0",
             "stat2", "aggr2", "var_rdy", "rstd", "nat_rdy", "nat_t", "x1b", "sc_ps", "mx", "sub", "exped", "summed", "rcp", "p_rdy",
             "p_t", "t_ev", "av", "wo_ps", "x2a", "x2_rdy", "z_hi", "z_lo", "mm", "sg_rdy", "v_rdy", "hi", "lo", "o_ev", "o_t", "fin1", "fin",
             "x1_in", "k_in", "v_in", "xr_in", "x2_st", "out_st", "vd_st", "step_v2", "step_s2", "raw_in", "checked", "folded", "col_st", "row_in", "flagged", "warm")
    S = {n: sem(n) for n in names}
    kd_st = [sem("kd_st0"), sem("kd_st1")]

    def blk_rows(d, i):
        return d.rearrange("(k j p) d -> k p j d", j=TPB, p=P)[bass.ds(i, 1)].rearrange("a p j d -> (a p) j d")

    w2v = a["w2"].rearrange("(u c p) k -> u p c k", c=4, p=P)
    w3v = a["w3"].rearrange("(u p) k -> u p k", p=P)
    xwv = a["xW"].rearrange("(c p) k -> p c k", p=P)

    raw_wide = [a[n].rearrange("(i p) k -> i p k", p=P) for n in ("h1", "h2")]
    raw_narrow = [a["w1"].rearrange("(i p) k -> i p k", p=P), a["w2"].rearrange("(i p) k -> i p k", p=P),
                  a["w3"].rearrange("(i r) (q k) -> i (r q) k", i=NBLK, q=4)]
    sg_flat = sg[:, :, :].rearrange("p a t -> p (a t)")
    CHECK = [10, 11, 12]

    TURN = [2, 5, 8, 11]
    VALUES_AT = [6, 12]
    block = ctx.enter_context(nc.Block())

    @block.sync
    def _(e):
        for u in range(2):
            e.dma_start(stage[u][:, :].rearrange("p (c k) -> p c k", c=4), w2v[u]).then_inc(w_in[u], 16)
        for b in range(BATCH):
            for d in range(2):
                e.dma_start(c2[64 * d:64 * d + 64, b, :], a["ctx"][b]).then_inc(S["c_in"], 16)
        e.dma_start(xbo[:, :], a["xb"].partition_broadcast(P)).then_inc(S["xbo_in"], 16)
        for u in range(2):
            e.wait_ge(S["pw_t"], u + 1)
            e.dma_start(stage[u][:, :], w3v[u]).then_inc(w_in[u], 16)
        e.wait_ge(S["pw_t"], 3)
        e.dma_start(stage[0][:, 0:512].rearrange("p (c k) -> p c k", c=2), xwv).then_inc(w_in[0], 16)
        e.wait_ge(S["vb_rdy"], 2)
        for k in range(2):
            e.dma_start(vd.rearrange("(b k) p m -> k p b m", k=2)[k], vst).then_inc(S["vd_st"], 16)
        for b in range(BATCH):
            e.wait_ge(S["kb_rdy"], 2 * (b + 1))
            for k in range(2):
                e.dma_start(kd[2 * b + k], kst[b % 2]).then_inc(kd_st[b % 2], 16)
        for s in kd_st:
            e.wait_ge(s, 64)
        e.wait_ge(S["vd_st"], 32)
        e.wait_ge(S["pw_t"], 5)

        def attn_loads(j):
            e.wait_ge(S["x2_st"], 16 * j)
            e.sem_inc(S["step_s2"], 1)
            e.wait_ge(S["nat_rdy"], 8 * j)
            e.dma_start(x1t[:, :].rearrange("p (j d) -> p j d", j=TPB), blk_rows(x1d, j)).then_inc(S["x1_in"], 16)
            e.wait_ge(S["sc_ps"], 4 * j)
            e.dma_start(kblk[:, :], kd[bass.ds(j, 1)].rearrange("a p k -> (a p) k")).then_inc(S["k_in"], 16)
            e.wait_ge(S["av"], 2 * j)
            e.dma_start(vblk[:, :], vd[bass.ds(j, 1)].rearrange("a p k -> (a p) k")).then_inc(S["v_in"], 16)

        def x2_store(j):
            e.wait_ge(S["x2_rdy"], j + 1)
            e.dma_start(blk_rows(x2d, j), x1t[:, :].rearrange("p (j d) -> p j d", j=TPB)).then_inc(S["x2_st"], 16)

        def res_load(i):
            e.wait_ge(S["x2_st"], 16 * i + 16)
            e.wait_ge(S["out_st"], 16 * i)
            e.dma_start(xr[:, :].rearrange("p (j d) -> p j d", j=TPB), blk_rows(x2d, i)).then_inc(S["xr_in"], 16)

        def raw_loads(i):
            for k, src in enumerate(raw_wide):
                e.wait_ge(*((S["v_rdy"], 8 * i + 8) if k == 0 else (S["checked"], 6 * i + 3)))
                e.dma_start(sg_flat, src[bass.ds(i, 1)].rearrange("a p k -> (a p) k")).then_inc(S["raw_in"], 16)
            e.wait_ge(S["checked"], 6 * i + 5)
            for k, src in enumerate(raw_narrow):
                e.dma_start(sg_flat[:, k * DM:(k + 1) * DM], src[bass.ds(i, 1)].rearrange("a p k -> (a p) k")).then_inc(S["raw_in"], 16)

        def out_store(i):
            e.wait_ge(S["fin"], i + 1)
            e.dma_start(blk_rows(a["out"].rearrange("b t d -> (b t) d"), i), xr[:, :].rearrange("p (j d) -> p j d", j=TPB)).then_inc(S["out_st"], 16)
        attn_loads(0)
        x2_store(0)
        attn_loads(1)
        with e.Fori(0, NBLK - 2) as i:
            res_load(i)
            raw_loads(i)
            x2_store(i + 1)
            attn_loads(i + 2)
            out_store(i)
        res_load(NBLK - 2)
        raw_loads(NBLK - 2)
        x2_store(NBLK - 1)
        out_store(NBLK - 2)
        res_load(NBLK - 1)
        raw_loads(NBLK - 1)
        e.wait_ge(S["folded"], 2)
        e.dma_start(t["flag_col"], most[:, :]).then_inc(S["col_st"], 16)
        e.wait_ge(S["col_st"], 16)
        e.dma_start(bit_row[:, :], t["flag_col"].rearrange("p o -> o p")).then_inc(S["row_in"], 16)
        out_store(NBLK - 1)
        e.wait_ge(S["out_st"], 16 * NBLK)

    @block.gpsimd
    def _(e):
        e.memset(hmask[:, :], 1.0).then_inc(S["mk"], 1)
        e.memset(mh, -0.5).then_inc(S["mk"], 1)
        e.wait_ge(S["mk"], 2)
        e.affine_select(out=hmask[:, :], in_=hmask[:, :], compare_op=ALU.is_ge, fill=0.0, base=0, pattern=[[-HD, 8]], channel_multiplier=1).then_inc(S["mk"], 1)
        e.wait_ge(S["mk"], 3)
        e.affine_select(out=hmask[:, :], in_=hmask[:, :], compare_op=ALU.is_ge, fill=0.0, base=HD - 1, pattern=[[HD, 8]], channel_multiplier=-1).then_inc(S["mk"], 1)
        e.wait_ge(S["xbo_in"], 16)

        def rstd(n):
            e.wait_ge(S["var_rdy"], n + 1)
            e.tensor_tensor(rs, ve, mh, ALU.pow).then_inc(S["rstd"], 1)

        def out_bias(j):
            e.wait_ge(S["nat_rdy"], 8 * j + 4)
            for m in range(TPB):
                v = x1t[:, m * DM:(m + 1) * DM]
                e.tensor_tensor(v, v, xbo[:, :], ALU.add).then_inc(S["x1b"], 1)

        def body(i, attn):
            if attn:
                rstd(2 * i + 2)
            for m in range(HC - 2):
                e.wait_ge(S["hi"], 24 * i + (m + 1))
                e.tensor_tensor(h1[1][:, m, :], vb[:, m % 2, :], h1[0][:, m, :], ALU.subtract).then_inc(S["lo"], 1)
            if attn:
                out_bias(i + 1)
                rstd(2 * i + 3)
        rstd(0)
        out_bias(0)
        rstd(1)
        with e.Fori(0, NBLK - 1) as i:
            body(i, True)
        body(NBLK - 1, False)

    @block.scalar
    def _(e):
        def w_evac(u, dst, src):
            e.wait_ge(S["pw_t"], u + 1)
            e.activation(dst, src, ACT.Copy).then_inc(S["pw_ev"], 1)
        for u in range(2):
            w_evac(u, w2T[:, :, 512 * u:512 * u + 512].rearrange("p k (c o) -> p c k o", c=4),
                   pair[u][:, :].rearrange("p (c k o) -> p c k o", c=4, k=DH))
        for u in range(2):
            w_evac(2 + u, w3T[:, :, P * u:P * (u + 1)], pair[u][:, :].rearrange("p (k o) -> p k o", k=HC))
        w_evac(4, xwoT[:, :, :].rearrange("p k (c o) -> p c k o", c=2), pair[0][:, 0:512].rearrange("p (c k o) -> p c k o", c=2, k=DH))

        def table(function, n):
            e.wait_ge(S["warm"], n)
            e.activation(warm[:, 1:2], warm[:, 0:1], function).then_inc(S["warm"], 1)

        def q_evac(j):
            e.wait_ge(S["nat_t"], 2 * j + 1)
            e.activation(qa[:, :, :].rearrange("p a t -> p (a t)"), pair[3][:, :], ACT.Copy).then_inc(S["t_ev"], 1)

        def exp(j, u, n):
            table(ACT.Exp, n)
            e.wait_ge(S["sub"], 4 * j + (u + 1))
            e.activation(prob[:, :, :], prob[:, :, :], ACT.Exp, scale=HD ** -0.5).then_inc(S["exped"], 1)

        def turn_evac(j, u):
            e.wait_ge(S["p_t"], 4 * j + (u + 1))
            first = u % 2 * 2 * P
            if u % 2 == 0:
                e.wait_ge(S["av"], 2 * j + u // 2)
            e.activation(pT[:, :, first:first + 2 * P].rearrange("p r (b t) -> p b r t", b=2),
                         pair[3][:, :].rearrange("p (b r t) -> p b r t", b=2, r=4), ACT.Copy).then_inc(S["t_ev"], 1)

        def av_evac(j, h):
            e.wait_ge(S["av"], 2 * j + (h + 1))
            e.activation(qa[:, h, :], t_ps[h], ACT.Copy).then_inc(S["t_ev"], 1)

        def z_evac(j):
            e.wait_ge(S["nat_t"], 2 * j + 2)
            e.activation(zT[0][:, :], pair[3][:, :], ACT.Copy).then_inc(S["z_hi"], 1)

        def gated(i, attn):
            for m in range(HC + 1):
                if attn and m == 5:
                    q_evac(i + 1)
                if m < HC:
                    e.wait_ge(S["mm"], 26 * i + (m + 1))
                    e.wait_ge(S["v_rdy"], 8 * i + max(m - 1, 0))
                    e.activation(sg[:, m % 2, :], pair[m % 2][:, 0:512], ACT.Silu, scale=sc1[:, m:m + 1]).then_inc(S["sg_rdy"], 1)
                if m > 0:
                    e.wait_ge(S["v_rdy"], 8 * i + m)
                    e.activation(h1[0][:, m - 1, :], vb[:, (m - 1) % 2, :], ACT.Copy).then_inc(S["hi"], 1)

        def hidden(i, s):
            dst = h2 if s < HC else h1
            m = s % HC
            sc = sch[s // HC][:, m:m + 1]
            e.wait_ge(S["mm"], 26 * i + (HC + s + 1))
            e.wait_ge(S["lo"], 24 * i + (HC + s - 1))
            e.activation(vb[:, s % 2, :], h_ps[s % 4], ACT.Gelu, scale=sc)
            e.activation(dst[0][:, m, :], h_ps[s % 4], ACT.Gelu, scale=sc).then_inc(S["hi"], 1)

        def out_evac(i, m):
            e.wait_ge(S["mm"], 26 * i + (25 + m))
            e.wait_ge(S["checked"], 6 * i + 7)
            e.activation(sg[:, m, :], h_ps[m], ACT.Copy, scale=sc3[:, m:m + 1]).then_inc(S["o_ev"], 1)

        def body(i, attn):
            j = i + 1
            gated(i, attn)
            turns = 9 * i + 4
            if attn:
                exp(j, 0, turns)
            table(ACT.Gelu, turns + (1 if attn else 0))
            for s in range(2 * HC):
                hidden(i, s)
                if attn and s in TURN:
                    u = TURN.index(s)
                    turn_evac(j, u)
                    if u < 3:
                        exp(j, u + 1, turns + (2 * u + 2))
                        table(ACT.Gelu, turns + (2 * u + 3))
                if attn and s in VALUES_AT:
                    av_evac(j, VALUES_AT.index(s))
            out_evac(i, 0)
            if attn:
                z_evac(j)
            out_evac(i, 1)
            if attn:
                table(ACT.Silu, turns + 8)
        q_evac(0)
        e.wait_ge(S["vb0"], 2)
        for u in range(4):
            exp(0, u, u)
            turn_evac(0, u)
            if u % 2 == 1:
                av_evac(0, u // 2)
        z_evac(0)
        with e.Fori(0, NBLK - 1) as i:
            body(i, True)
        body(NBLK - 1, False)

    @block.vector
    def _(e):
        e.memset(vst, 0.0).then_inc(S["vb0"], 1)
        e.memset(warm[:, :], 0.0).then_inc(S["vb0"], 1)
        e.memset(bits[:, :], 0).then_inc(S["checked"], 1)
        e.wait_ge(S["vb0"], 2)
        e.wait_ge(S["c_in"], 128)
        for h in range(2):
            dv = vst[64 * h:64 * h + 64].rearrange("p b (r g d) -> p (b r) g d", r=8, g=2)[:, :, h, :]
            sv = c2[64 * h:64 * h + 64].rearrange("p b (r g d) -> p (b r) g d", r=8, g=2)[:, :, h, :]
            e.tensor_copy(dv, sv).then_inc(S["vb_rdy"], 1)
        e.wait_ge(S["pc_t"], 1)
        e.wait_ge(S["mk"], 4)
        for b in range(BATCH):
            if b >= 2:
                e.wait_ge(kd_st[b % 2], 32)
            for h in range(2):
                src = pair[3][:, (2 * b + h) * KEYS:(2 * b + h + 1) * KEYS].unsqueeze(1).to_broadcast([P, 8, KEYS])
                dst = kst[b % 2][:, h * BLK:(h + 1) * BLK].rearrange("p (g k) -> p g k", g=8)
                e.tensor_tensor(dst, src, hmask[:, :].unsqueeze(2).to_broadcast([P, 8, KEYS]), ALU.mult).then_inc(S["kb_rdy"], 1)
        for s in kd_st:
            e.wait_ge(s, 64)

        def stats(n):
            for m in range(TPB):
                e.bn_stats(st[:, m, :], x1t[:, m * DM:(m + 1) * DM]).then_inc(S["stat2"], 1)
            e.wait_ge(S["stat2"], 4 * n + 4)
            e.wait_ge(S["nat_rdy"], 4 * n)
            e.sem_inc(S["step_v2"], 1)
            for m in range(TPB):
                e.bn_aggr(mv[:, m, :], st[:, m, :]).then_inc(S["aggr2"], 1)
            e.wait_ge(S["aggr2"], 4 * n + 4)
            e.tensor_scalar_add(ve, mv[:, :, 1], EPS).then_inc(S["var_rdy"], 1)

        def normed(n):
            e.wait_ge(S["rstd"], n + 1)
            e.wait_ge(S["nat_t"], n)
            for m in range(TPB):
                e.tensor_scalar(nat[:, m, :], x1t[:, m * DM:(m + 1) * DM], mv[:, m, 0:1], rs[:, m:m + 1], ALU.subtract, ALU.mult).then_inc(S["nat_rdy"], 1)

        def pairwise(v):
            return v.rearrange("p b (h k) -> p b h k", h=8)
        s4 = pair[2][:, :].rearrange("p (b h k) -> p b h k", b=2, h=8)
        p4 = pairwise(prob[:, :, :])

        def spread(k):
            return red[:, k, :, :].unsqueeze(3).to_broadcast([P, 2, 8, KEYS])

        def maxima(j, u):
            e.wait_ge(S["sc_ps"], 4 * j + (u + 1))
            e.tensor_reduce(red[:, 0, :, :], s4, AX.X, ALU.max).then_inc(S["mx"], 1)

        def shifted(j, u):
            e.wait_ge(S["mx"], 4 * j + (u + 1))
            if u > 0:
                e.wait_ge(S["p_t"], 4 * j + u)
            e.tensor_tensor(p4, s4, spread(0), ALU.subtract).then_inc(S["sub"], 1)

        def normalised(j, u):
            e.wait_ge(S["exped"], 4 * j + (u + 1))
            e.tensor_reduce(red[:, 1, :, :], p4, AX.X, ALU.add).then_inc(S["summed"], 1)
            e.wait_ge(S["summed"], 4 * j + (u + 1))
            e.reciprocal(red[:, 2, :, :], red[:, 1, :, :]).then_inc(S["rcp"], 1)
            e.wait_ge(S["rcp"], 4 * j + (u + 1))
            e.tensor_tensor(p4, p4, spread(2), ALU.mult).then_inc(S["p_rdy"], 1)

        def residual(j):
            e.wait_ge(S["wo_ps"], j + 1)
            e.wait_ge(S["x1b"], 4 * j + 4)
            e.tensor_tensor(x1t[:, :], pair[3][:, :], x1t[:, :], ALU.add).then_inc(S["x2_rdy"], 1)
            e.wait_ge(S["x2_rdy"], j + 1)

        def z_lo(j):
            e.wait_ge(S["z_hi"], j + 1)
            e.tensor_tensor(zT[1][:, :], pair[3][:, :], zT[0][:, :], ALU.subtract).then_inc(S["z_lo"], 1)

        def low(i, n, dst):
            e.wait_ge(S["hi"], 24 * i + (n + 1))
            e.tensor_tensor(dst[1][:, n % HC, :], vb[:, n % 2, :], dst[0][:, n % HC, :], ALU.subtract).then_inc(S["lo"], 1)

        def checked(i, k):
            e.wait_ge(S["raw_in"], 80 * i + (16, 32, 80)[k])
            for half, n in enumerate((BLK, 3 * DM - BLK if k == 2 else BLK)):
                e.wait_ge(S["checked"], 6 * i + (2 * k + half + 1))
                e.tensor_tensor(bits[:, 0:n], bits[:, 0:n], sg[:, half, 0:n].bitcast(I32), ALU.bitwise_or).then_inc(S["checked"], 1)

        def body(i, attn):
            j = i + 1
            if attn:
                e.wait_ge(S["x1_in"], 16 * j + 16)
                stats(2 * j)
            for m in range(HC):
                e.wait_ge(S["sg_rdy"], 8 * i + (m + 1))
                e.wait_ge(S["lo"], 24 * i + max(m - 1, 0))
                e.scalar_tensor_tensor(vb[:, m % 2, :], pair[m % 2][:, 512:1024], sc2[:, m:m + 1], sg[:, m % 2, :],
                                       ALU.mult, ALU.mult).then_inc(S["v_rdy"], 1)
                if m == HC - 1:
                    e.wait_ge(S["lo"], 24 * i + m - 1)
                    low(i, m - 1, h1)
                    low(i, m, h1)
                if attn and m == 1:
                    normed(2 * j)
            if attn:
                maxima(j, 0)
                shifted(j, 0)
            for s in range(2 * HC):
                low(i, HC + s, h2 if s < HC else h1)
                if attn and s in TURN and s != TURN[3]:
                    shifted(j, TURN.index(s) + 1)
                if attn and s + 1 in TURN and s + 1 != TURN[3]:
                    maxima(j, TURN.index(s + 1) + 1)
                if attn and s + 2 in TURN:
                    normalised(j, TURN.index(s + 2))
                if attn and s == 13:
                    residual(j)
                    stats(2 * j + 1)
                if attn and s == 14:
                    normed(2 * j + 1)
                if s in CHECK:
                    checked(i, CHECK.index(s))
            if attn:
                z_lo(j)
            else:
                e.wait_ge(S["checked"], 6 * NBLK + 1)
                e.tensor_scalar(bits[:, :], bits[:, :], 0xFFF, None, ALU.bitwise_and).then_inc(S["folded"], 1)
                e.wait_ge(S["folded"], 1)
                e.tensor_reduce(most[:, :], bits[:, :], AX.X, ALU.max).then_inc(S["folded"], 1)
                e.wait_ge(S["row_in"], 16)
                e.tensor_reduce(t["flag"][:, :], bit_row[:, :], AX.X, ALU.max).then_inc(S["flagged"], 1)
            e.wait_ge(S["o_t"], i + 1)
            e.wait_ge(S["xr_in"], 16 * i + 16)
            e.tensor_tensor(xr[:, :], pair[2][:, :], xr[:, :], ALU.add).then_inc(S["fin"], 1)
        e.wait_ge(S["x1_in"], 16)
        stats(0)
        normed(0)
        maxima(0, 0)
        for u in range(4):
            shifted(0, u)
            if u < 3:
                maxima(0, u + 1)
            normalised(0, u)
        residual(0)
        stats(1)
        normed(1)
        z_lo(0)
        with e.Fori(0, NBLK - 1) as i:
            body(i, True)
        body(NBLK - 1, False)

    @block.tensor
    def _(e):
        for u in range(5):
            e.wait_ge(w_in[u % 2], 16 * (u // 2 + 1))
            if u >= 2:
                e.wait_ge(S["pw_ev"], u - 1)
            for n in range(8 if u < 4 else 4):
                ins = e.transpose(pair[u % 2][:, n * P:(n + 1) * P], stage[u % 2][:, n * P:(n + 1) * P], ident[:, :])
            ins.then_inc(S["pw_t"], 1)
        e.wait_ge(S["c_in"], 128)
        for b in range(BATCH):
            for h in range(2):
                ins = e.transpose(pair[3][:, (2 * b + h) * KEYS:(2 * b + h + 1) * KEYS], c2[0:KEYS, b, h * P:(h + 1) * P], ident[0:KEYS, 0:KEYS])
        ins.then_inc(S["pc_t"], 1)
        e.wait_ge(S["pw_ev"], 5)

        def turn_nat(n):
            e.wait_ge(S["nat_rdy"], 4 * n + 4)
            for k in range(DH):
                for m in range(TPB):
                    ins = e.transpose(pair[3][:, k * BLK + m * P:k * BLK + (m + 1) * P], nat[:, m, k * P:(k + 1) * P], ident[:, :])
            ins.then_inc(S["nat_t"], 1)

        def turn_q(j):
            e.wait_ge(S["z_lo"], j)
            turn_nat(2 * j)

        def turn_z(j):
            e.wait_ge(S["x2_rdy"], j + 1)
            turn_nat(2 * j + 1)

        def scores(j, u):
            if u == 0:
                e.wait_ge(S["t_ev"], 7 * j + 1)
                e.wait_ge(S["k_in"], 16 * j + 16)
                if not isinstance(j, int):
                    e.wait_ge(S["fin"], j - 1)
            else:
                e.wait_ge(S["sub"], 4 * j + u)
            h = u // 2
            for b in range(2):
                tile = 2 * (u % 2) + b
                ins = e.matmul(pair[2][:, b * BLK:(b + 1) * BLK], qa[:, h, tile * P:(tile + 1) * P], kblk[:, h * BLK:(h + 1) * BLK], start=True, stop=True)
            ins.then_inc(S["sc_ps"], 1)

        def turn_p(j, u):
            e.wait_ge(S["p_rdy"], 4 * j + (u + 1))
            e.wait_ge(S["t_ev"], 7 * j + (1 + u + u // 2))
            for b in range(2):
                for r in range(4):
                    ins = e.transpose(pair[3][:, b * BLK + r * P:b * BLK + (r + 1) * P], prob[:, b, r * P:(r + 1) * P], ident[:, :])
            ins.then_inc(S["p_t"], 1)

        def values(j, h):
            if h == 0:
                e.wait_ge(S["v_in"], 16 * j + 16)
            e.wait_ge(S["t_ev"], 7 * j + (3 if h == 0 else 6))
            for r in range(4):
                c = (4 * h + r) * 32
                ins = e.matmul(t_ps[h][32 * r:32 * r + 32, :], vblk[:, c:c + 32], pT[:, r, :], start=True, stop=True)
            ins.then_inc(S["av"], 1)

        def project(j):
            e.wait_ge(S["t_ev"], 7 * j + 7)
            for m in range(TPB):
                for k in range(DH):
                    ins = e.matmul(pair[3][:, m * DM:(m + 1) * DM], qa[:, k, m * P:(m + 1) * P], xwoT[:, k, :], start=(k == 0), stop=(k == DH - 1))
            ins.then_inc(S["wo_ps"], 1)

        def gated(i, m):
            if m == 0:
                e.wait_ge(S["z_lo"], i + 1)
                e.wait_ge(S["o_ev"], 2 * i)
            elif m >= 2:
                e.wait_ge(S["v_rdy"], 8 * i + (m - 1))
            for g, w in enumerate((w1T, w2T)):
                for k in range(DH):
                    for part in range(2):
                        ins = e.matmul(pair[m % 2][:, 512 * g:512 * g + 512], w[:, k, m * P:(m + 1) * P], zT[part][:, k * BLK:(k + 1) * BLK],
                                       start=(k == 0 and part == 0), stop=(k == DH - 1 and part == 1))
            ins.then_inc(S["mm"], 1)

        def product(i, s, w, src, bank):
            m = s % HC
            for k in range(HC):
                if m == 0:
                    e.wait_ge(S["lo"], 24 * i + (HC * (s // HC) + k + 1))
                for part in range(2):
                    ins = e.matmul(bank, w[:, k, m * P:(m + 1) * P], src[part][:, k, :],
                                   start=(k == 0 and part == 0), stop=(k == HC - 1 and part == 1))
            ins.then_inc(S["mm"], 1)

        def hidden(i, s):
            if s < 2:
                e.wait_ge(S["v_rdy"], 8 * i + 7)
            elif s < 4:
                e.wait_ge(S["v_rdy"], 8 * i + 8)
            else:
                e.wait_ge(S["hi"], 24 * i + (HC + s - 3))
            product(i, s, h1T if s < HC else h2T, h1 if s < HC else h2, h_ps[s % 4])

        def last(i, m):
            e.wait_ge(S["hi"], 24 * i + (21 + m))
            product(i, 16 + m, w3T, h1, h_ps[m])

        def turn_out(i):
            for k in range(DH):
                e.wait_ge(S["o_ev"], 2 * i + (k + 1))
                for m in range(TPB):
                    ins = e.transpose(pair[2][:, m * DM + k * P:m * DM + (k + 1) * P], sg[:, k, m * P:(m + 1) * P], ident[:, :])
            ins.then_inc(S["o_t"], 1)

        def body(i, attn):
            j = i + 1
            for m in range(HC):
                gated(i, m)
                if attn and m == 3:
                    turn_q(j)
                if attn and m == 6:
                    scores(j, 0)
            for s in range(2 * HC):
                hidden(i, s)
                if attn and s in TURN:
                    turn_p(j, TURN.index(s))
                if attn and s + 2 in TURN and s + 2 != TURN[3]:
                    scores(j, TURN.index(s + 2) + 1)
                if attn and s in VALUES_AT:
                    values(j, VALUES_AT.index(s))
                if attn and s == 13:
                    project(j)
            last(i, 0)
            if attn:
                turn_z(j)
            last(i, 1)
            turn_out(i)
        turn_q(0)
        scores(0, 0)
        for u in range(4):
            if u < 3:
                scores(0, u + 1)
            turn_p(0, u)
            if u % 2 == 1:
                values(0, u // 2)
        project(0)
        turn_z(0)
        with e.Fori(0, NBLK - 1) as i:
            body(i, True)
        body(NBLK - 1, False)


def exact_weights_program(nc, ctx, a, t):
    def sb(name, shape, dt=F32):
        return ctx.enter_context(nc.sbuf_tensor(name, shape, dt))

    def sem(name):
        return ctx.enter_context(nc.semaphore(name))

    turned = {"w1": sb("w1X", [P, DH, HID]), "w2": sb("w2X", [P, DH, HID]), "w3": sb("w3X", [P, HC, DM]),
              "h1": sb("h1X", [P, HC, HID]), "h2": sb("h2X", [P, HC, HID])}
    stage = [sb("stageX0", [P, 1024]), sb("stageX1", [P, 1024])]
    ha = sb("haX", [P, HC, BLK])
    hb = sb("hbX", [P, HC, BLK])
    zT = sb("zTX", [P, DH * BLK])
    xt = sb("xtX", [P, TPB * DM])
    nat = sb("natX", [P, TPB, DM])
    sg = sb("sgX", [P, 2, BLK])
    st = sb("stX", [P, TPB, 6])
    mv = sb("mvX", [P, TPB, 2])
    lnv = sb("lnvX", [P, 3, TPB])
    ve, rs, mh = lnv[:, 0, :], lnv[:, 1, :], lnv[:, 2, :]
    pair, ident, scl = t["pair"], t["ident"], t["scl"]
    h_ps = [pair[k // 2][:, 512 * (k % 2):512 * (k % 2) + 512] for k in range(4)]
    sc1, sc2, sch, sc3 = scl[:, 0:8], scl[:, 8:16], (scl[:, 16:24], scl[:, 24:32]), scl[:, 32:34]
    w_in = [sem("xw_in0"), sem("xw_in1")]
    w_t, w_ev, x_in, half, stat, aggr, var_rdy, rstd, nat_rdy, nat_t, z_rdy = (sem("x" + n) for n in (
        "w_t", "w_ev", "x_in", "half", "stat", "aggr", "var_rdy", "rstd", "nat_rdy", "nat_t", "z_rdy"))
    mm, sg_rdy, gate_rdy, act_rdy, o_ev, o_t, fin, out_st, step_v, step_t = (sem("x" + n) for n in (
        "mm", "sg_rdy", "gate_rdy", "act_rdy", "o_ev", "o_t", "fin", "out_st", "step_v", "step_t"))

    def rows(d, i):
        return d.rearrange("(k j p) d -> k p j d", j=TPB, p=P)[bass.ds(i, 1)].rearrange("a p j d -> (a p) j d")
    xt3 = xt[:, :].rearrange("p (j d) -> p j d", j=TPB)
    natural = {n: a[n].rearrange("(u c p) k -> u p c k", c=4, p=P) for n in ("w1", "w2")}
    natural.update({n: a[n].rearrange("(u p) k -> u p k", p=P) for n in ("w3", "h1", "h2")})
    NARROW, WIDE = (("w1", 0), ("w2", 2), ("w3", 4)), (("h1", 6), ("h2", 6 + HC))

    block = ctx.enter_context(nc.Block())

    def needed(e):
        return e.value_load(t["flag"][0:1, 0:1], min_val=0, max_val=0xFFF) > 0

    @block.sync
    def _(e):
        with e.If(needed(e)):
            for n, base in NARROW:
                for u in range(2):
                    if base > 0:
                        e.wait_ge(w_t, base + u - 1)
                    dst = stage[u][:, :].rearrange("p (c k) -> p c k", c=4) if n != "w3" else stage[u][:, :]
                    e.dma_start(dst, natural[n][u]).then_inc(w_in[u], 16)
            for n, base in WIDE:
                with e.Fori(0, HC // 2) as k:
                    for q in range(2):
                        e.wait_ge(w_t, 2 * k + (base + q - 1))
                        e.dma_start(stage[q][:, :], natural[n][bass.ds(2 * k + q, 1)].rearrange("a p k -> (a p) k")).then_inc(w_in[q], 16)
            with e.Fori(0, NBLK) as i:
                e.wait_ge(out_st, 16 * i)
                e.dma_start(xt3, rows(t["x2d"], i)).then_inc(x_in, 16)
                e.wait_ge(fin, i + 1)
                e.dma_start(rows(a["out"].rearrange("b t d -> (b t) d"), i), xt3).then_inc(out_st, 16)
            e.wait_ge(out_st, 16 * NBLK)

    @block.gpsimd
    def _(e):
        with e.If(needed(e)):
            e.memset(mh, -0.5).then_inc(half, 1)
            e.wait_ge(half, 1)
            with e.Fori(0, NBLK) as i:
                e.wait_ge(var_rdy, i + 1)
                e.tensor_tensor(rs, ve, mh, ALU.pow).then_inc(rstd, 1)

    @block.scalar
    def _(e):
        with e.If(needed(e)):
            for n, base in NARROW:
                for u in range(2):
                    e.wait_ge(w_t, base + u + 1)
                    if n == "w3":
                        e.activation(turned[n][:, :, P * u:P * (u + 1)], pair[u][:, :].rearrange("p (k o) -> p k o", k=HC), ACT.Copy).then_inc(w_ev, 1)
                    else:
                        e.activation(turned[n][:, :, 512 * u:512 * u + 512].rearrange("p k (c o) -> p c k o", c=4),
                                     pair[u][:, :].rearrange("p (c k o) -> p c k o", c=4, k=DH), ACT.Copy).then_inc(w_ev, 1)
            for n, base in WIDE:
                with e.Fori(0, HC // 2) as k:
                    for q in range(2):
                        e.wait_ge(w_t, 2 * k + (base + q + 1))
                        e.activation(turned[n][:, :, bass.ds(2 * P * k + P * q, P)], pair[q][:, :].rearrange("p (k o) -> p k o", k=HC), ACT.Copy).then_inc(w_ev, 1)
            with e.Fori(0, NBLK) as i:
                e.wait_ge(nat_t, i + 1)
                e.activation(zT[:, :], pair[3][:, :], ACT.Copy).then_inc(z_rdy, 1)
                for m in range(HC):
                    e.wait_ge(mm, 26 * i + (m + 1))
                    e.wait_ge(gate_rdy, 8 * i + max(m - 1, 0))
                    e.activation(sg[:, m % 2, :], pair[m % 2][:, 0:512], ACT.Silu, scale=sc1[:, m:m + 1]).then_inc(sg_rdy, 1)
                for s in range(2 * HC):
                    m = s % HC
                    e.wait_ge(mm, 26 * i + (HC + s + 1))
                    e.activation((hb if s < HC else ha)[:, m, :], h_ps[s % 4], ACT.Gelu, scale=sch[s // HC][:, m:m + 1]).then_inc(act_rdy, 1)
                for m in range(DH):
                    e.wait_ge(mm, 26 * i + (25 + m))
                    e.activation(sg[:, m, :], h_ps[m], ACT.Copy, scale=sc3[:, m:m + 1]).then_inc(o_ev, 1)

    @block.vector
    def _(e):
        with e.If(needed(e)):
            with e.Fori(0, NBLK) as i:
                e.wait_ge(x_in, 16 * i + 16)
                for m in range(TPB):
                    e.bn_stats(st[:, m, :], xt[:, m * DM:(m + 1) * DM]).then_inc(stat, 1)
                e.wait_ge(stat, 4 * i + 4)
                e.sem_inc(step_v, 1)
                for m in range(TPB):
                    e.bn_aggr(mv[:, m, :], st[:, m, :]).then_inc(aggr, 1)
                e.wait_ge(aggr, 4 * i + 4)
                e.tensor_scalar_add(ve, mv[:, :, 1], EPS).then_inc(var_rdy, 1)
                e.wait_ge(rstd, i + 1)
                for m in range(TPB):
                    e.tensor_scalar(nat[:, m, :], xt[:, m * DM:(m + 1) * DM], mv[:, m, 0:1], rs[:, m:m + 1], ALU.subtract, ALU.mult).then_inc(nat_rdy, 1)
                for m in range(HC):
                    e.wait_ge(sg_rdy, 8 * i + (m + 1))
                    e.scalar_tensor_tensor(ha[:, m, :], pair[m % 2][:, 512:1024], sc2[:, m:m + 1], sg[:, m % 2, :], ALU.mult, ALU.mult).then_inc(gate_rdy, 1)
                e.wait_ge(o_t, i + 1)
                e.tensor_tensor(xt[:, :], pair[1][:, :], xt[:, :], ALU.add).then_inc(fin, 1)

    @block.tensor
    def _(e):
        with e.If(needed(e)):
            for n, base in NARROW:
                for u in range(2):
                    e.wait_ge(w_in[u], 8 * base + 16)
                    if base > 0:
                        e.wait_ge(w_ev, base + u - 1)
                    for c in range(HC):
                        ins = e.transpose(pair[u][:, c * P:(c + 1) * P], stage[u][:, c * P:(c + 1) * P], ident[:, :])
                    ins.then_inc(w_t, 1)
            for n, base in WIDE:
                with e.Fori(0, HC // 2) as k:
                    for q in range(2):
                        e.wait_ge(w_in[q], 16 * k + (8 * base + 16))
                        e.wait_ge(w_ev, 2 * k + (base + q - 1))
                        for c in range(HC):
                            ins = e.transpose(pair[q][:, c * P:(c + 1) * P], stage[q][:, c * P:(c + 1) * P], ident[:, :])
                        ins.then_inc(w_t, 1)
            e.wait_ge(w_ev, 6 + 2 * HC)

            def product(w, src, m, chunks, bank):
                for k in range(chunks):
                    ins = e.matmul(bank, w[:, k, m * P:(m + 1) * P], src(k), start=(k == 0), stop=(k == chunks - 1))
                return ins
            with e.Fori(0, NBLK) as i:
                e.wait_ge(nat_rdy, 4 * i + 4)
                for k in range(DH):
                    for m in range(TPB):
                        ins = e.transpose(pair[3][:, k * BLK + m * P:k * BLK + (m + 1) * P], nat[:, m, k * P:(k + 1) * P], ident[:, :])
                ins.then_inc(nat_t, 1)
                for m in range(HC):
                    if m == 0:
                        e.wait_ge(z_rdy, i + 1)
                        e.wait_ge(o_ev, 2 * i)
                    elif m == 1:
                        e.wait_ge(fin, i)
                    else:
                        e.wait_ge(gate_rdy, 8 * i + (m - 1))
                    for g, n in enumerate(("w1", "w2")):
                        ins = product(turned[n], lambda k: zT[:, k * BLK:(k + 1) * BLK], m, DH, pair[m % 2][:, 512 * g:512 * g + 512])
                    ins.then_inc(mm, 1)
                for s in range(2 * HC):
                    if s == 0:
                        e.wait_ge(gate_rdy, 8 * i + 8)
                    elif s == HC:
                        e.wait_ge(act_rdy, 16 * i + HC)
                    elif s >= 4:
                        e.wait_ge(act_rdy, 16 * i + (s - 3))
                    src = ha if s < HC else hb
                    product(turned["h1" if s < HC else "h2"], lambda k: src[:, k, :], s % HC, HC, h_ps[s % 4]).then_inc(mm, 1)
                for m in range(DH):
                    e.wait_ge(act_rdy, 16 * i + 2 * HC)
                    product(turned["w3"], lambda k: ha[:, k, :], m, HC, h_ps[m]).then_inc(mm, 1)
                e.wait_ge(o_ev, 2 * i + 2)
                for m in range(TPB):
                    for k in range(DH):
                        ins = e.transpose(pair[1][:, m * DM + k * P:m * DM + (k + 1) * P], sg[:, k, m * P:(m + 1) * P], ident[:, :])
                ins.then_inc(o_t, 1)


def decoder_layer(nc, a):
    with ExitStack() as ctx:
        t = {}
        t["ident"] = ctx.enter_context(nc.sbuf_tensor("ident", [P, P], F32))
        t["scl"] = ctx.enter_context(nc.sbuf_tensor("scl", [P, 4 * HC + DH], F32))
        t["pair"] = [ctx.enter_context(nc.psum_tensor(f"pair{k}", [P, 1024], F32)) for k in range(4)]
        t["flag"] = ctx.enter_context(nc.sbuf_tensor("flag", [1, 1], I32))
        kr_h = nc.dram_tensor("kernel_rows", [1, DM * L + L], F32, kind="Internal")
        al_h = nc.dram_tensor("alpha_rows", [DM, N], F32, kind="Internal")
        t["kr_h"], t["kr"], t["alS_h"], t["alS"] = kr_h, kr_h.ap(), al_h, al_h.ap()
        t["flag_col"] = nc.dram_tensor("flag_column", [P, 1], I32, kind="Internal").ap()
        t["x1d"] = nc.dram_tensor("x1_rows", [TOK, DM], F32, kind="Internal").ap()
        t["x2d"] = nc.dram_tensor("x2_rows", [TOK, DM], F32, kind="Internal").ap()
        t["kd"] = nc.dram_tensor("key_blocks", [NBLK, P, 2 * BLK], F32, kind="Internal").ap()
        t["vd"] = nc.dram_tensor("value_blocks", [NBLK, P, DM], F32, kind="Internal").ap()
        with ExitStack() as shared:
            t["w1T"] = shared.enter_context(nc.sbuf_tensor("w1T", [P, DH, HID], F32R))
            t["h1T"] = shared.enter_context(nc.sbuf_tensor("h1T", [P, HC, HID], F32R))
            t["h2T"] = shared.enter_context(nc.sbuf_tensor("h2T", [P, HC, HID], F32R))
            with ExitStack() as one:
                mixer_program(nc, one, a, t)
            with ExitStack() as two:
                attention_ffn_program(nc, two, a, t)
        with ExitStack() as three:
            exact_weights_program(nc, three, a, t)


_NAMES = {"x": "x", "ctx_1024": "ctx", "L0_attn_log_A": "logA", "L0_attn_B_param": "Bp", "L0_attn_C_param": "Cp",
          "L0_attn_D_param": "Dp", "L0_attn_log_dt": "log_dt", "L0_attn_ln_gamma": "gamma", "L0_attn_ln_beta": "beta",
          "L0_attn_W_out": "aW", "L0_attn_b_out": "ab", "L0_xattn_W_out": "xW", "L0_xattn_b_out": "xb",
          "L0_ffn_w1_w": "w1", "L0_ffn_w1_s": "s1", "L0_ffn_w2_w": "w2", "L0_ffn_w2_s": "s2", "L0_ffn_h1_w": "h1",
          "L0_ffn_h1_s": "hs1", "L0_ffn_h2_w": "h2", "L0_ffn_h2_s": "hs2", "L0_ffn_w3_w": "w3", "L0_ffn_w3_s": "s3"}


def kernel(**inputs):
    import concourse.bacc as _bacc
    from concourse.bass_utils import run_bass_kernel_spmd as _run

    nc = _bacc.Bacc("TRN2", target_bir_lowering=False, num_devices=1)
    arrays, aps = {}, {}
    for name, short in _NAMES.items():
        v = np.ascontiguousarray(inputs[name])
        arrays[f"in_{short}"] = v
        aps[short] = nc.dram_tensor(f"in_{short}", v.shape, mybir.dt.from_np(v.dtype), kind="ExternalInput").ap()
    aps["out"] = nc.dram_tensor("out", (BATCH, T, DM), F32, kind="ExternalOutput").ap()
    decoder_layer(nc, aps)
    r = _run(nc, [arrays], core_ids=[0])
    return r.results[0]["out"]
```

```python
import numpy as np
import concourse.bass as bass
from concourse import mybir
from contextlib import ExitStack

F32 = mybir.dt.float32
F32R = mybir.dt.float32r
I32 = mybir.dt.int32
ACT = mybir.ActivationFunctionType
ALU = mybir.AluOpType
AX = mybir.AxisListType

P = 128
BATCH, T, DM = 4, 1024, 256
N = 64
L = 64
CH = T // L
BC = BATCH * CH
TOK = BATCH * T
TILES = TOK // P
KEYS, HEADS, HD = 64, 16, 16
HID = 1024
BLK = 512
NBLK = TOK // BLK
TPB = BLK // P
EPS = 1e-5
DH = DM // P
HC = HID // P
OCT = 8
GRP = 16
NGRP = DM // GRP


def mixer_program(nc, ctx, a, t):
    def sb(name, shape, dt=F32):
        return ctx.enter_context(nc.sbuf_tensor(name, shape, dt))

    def sem(name):
        return ctx.enter_context(nc.semaphore(name))

    V = sb("V", [P, DM, BC])
    Vf = V[:, :, :].rearrange("p d c -> p (d c)")
    V4 = V[:, :, :].rearrange("p d (b c) -> p d b c", b=BATCH)
    xres = sb("xres", [P, TILES, DM])
    ring = sb("ring", [P, 4096])
    dec = sb("dec", [P, 2, OCT * BC])
    zt = dec[:, :, :].rearrange("p a (b m) -> p (a b) m", b=2)
    stage = sb("stage", [P, 2, 1024])
    gam = sb("gam", [P, DM])
    bet = sb("bet", [P, DM])
    bo = sb("bo", [P, DM])
    a64 = sb("a64", [N, DM])
    woT = sb("woT", [P, DH, DM])
    rev = sb("rev", [P, P])
    ones = sb("ones", [P, 32])
    esc = sb("esc", [L, 1])
    st = sb("st", [P, 4, 6])
    mv4 = sb("mv4", [P, 2, 4, 2])
    sv = sb("sv", [P, 2, TILES])
    rs = sb("rs", [P, 2, TILES])
    ng = sb("ng", [P, 2, TILES])
    mhalf = sb("mhalf", [P, 2, 4])
    edit = sb("edit", [P, 2, DM])
    dtc = sb("dtc", [P, 4])
    pk = ring[:, 0:6 * P].rearrange("p (k d) -> p k d", k=6)
    ksb = ring[:, 0:2048].rearrange("p (a m) -> p a m", a=4)
    natA = ring[:, 3072:3200].rearrange("p (h n) -> p h n", h=DH)
    natB = ring[:, 3200:3328].rearrange("p (h n) -> p h n", h=DH)
    natC = ring[:, 3328:3456].rearrange("p (h n) -> p h n", h=DH)
    al3 = ring[:, 3456:3648].rearrange("p (u n) -> p u n", u=3)
    w10 = ring[:, 3712:3840].rearrange("p (u n) -> p u n", u=2)
    TG = [ring[:, 1024 * k:1024 * (k + 1)] for k in range(2)]
    EE = [ring[:, 1024 * (2 + k):1024 * (3 + k)] for k in range(2)]
    yT = [ring[:, 1024 * k:1024 * (k + 1)] for k in range(2)]
    zb = [ring[:, 1024 * (2 + k):1024 * (3 + k)] for k in range(2)]
    pair = t["pair"]
    alT = pair[3][:, 0:DM]
    wT = pair[3][:, 512:512 + P]
    hps = [pair[1][:, 512 * k:512 * (k + 1)] for k in range(2)]
    yps = [pair[2][:, 512 * k:512 * (k + 1)] for k in range(2)]
    kps = [pair[3][:, 512 * k:512 * (k + 1)] for k in range(2)]
    wps = [pair[0], pair[2]]
    ident = t["ident"]
    kr, alS, x1d = t["kr"], t["alS"], t["x1d"]
    ahead_w2 = [t[n][:, :, :].rearrange("p a (c k) -> p (a c) k", c=2) for n in ("vb", "sg")]
    context = ahead_w2[0][0:KEYS]

    coef_in, bc_in, x_in, d_in, scl_in = (sem(n) for n in ("coef_in", "bc_in", "x_in", "d_in", "scl_in"))
    const, exps, coef, al_st = sem("const"), sem("exps"), sem("coef"), sem("al_st")
    coef_t, pk_done, g_row, k_ps, k_ev, d_add = (sem(n) for n in ("coef_t", "pk_done", "g_row", "k_ps", "k_ev", "d_add"))
    kr_st = [sem(f"kr_st{k}") for k in range(4)]
    kr_pad = sem("kr_pad")
    nm_rdy, stat, aggr, var_rdy, powd, z_rdy, z_g, zt_free = (sem(n) for n in ("nm_rdy", "stat", "aggr", "var_rdy", "powd", "z_rdy", "z_g", "zt_free"))
    w_in = [sem("w_in0"), sem("w_in1")]
    w_t, w_ev = sem("w_t"), sem("w_ev")
    A_in, T_in = [sem("A_in0"), sem("A_in1")], [sem("T_in0"), sem("T_in1")]
    t_mask, e_rdy, g_cp, h_ps, h_scan, dec_rdy = (sem(n) for n in ("t_mask", "e_rdy", "g_cp", "h_ps", "h_scan", "dec_rdy"))
    y_ps, y_out, dec0, ezero = sem("y_ps"), sem("y_out"), sem("dec0"), sem("ezero")
    y_t, y_tev, pr_ps, zb_rdy, zb_b, x1a, x1_rdy = (sem(n) for n in ("y_t", "y_tev", "pr_ps", "zb_rdy", "zb_b", "x1a", "x1_rdy"))
    x1_st = [sem("x1_st0"), sem("x1_st1")]
    g_moved = sem("g_moved")
    c_in, c_t, c_ev, ahead = sem("c_in"), sem("c_t"), sem("c_ev"), sem("ahead")
    step_v, step_t, step_g = (sem(n) for n in ("step_v", "step_t", "step_g"))

    w1v = a["w1"].rearrange("(u c p) k -> u p c k", c=4, p=P)
    h1v = a["h1"].rearrange("(u p) k -> u p k", p=P)
    awv = a["aW"].rearrange("(c p) k -> p c k", p=P)
    xv = a["x"].rearrange("b t d -> (b t) d").rearrange("(k j p) d -> k p j d", j=4, p=P)
    x1v = x1d.rearrange("(k j p) d -> k p j d", j=4, p=P)
    NW = 3 + HC
    EARLY = 5

    def tg_load(e, g, p):
        e.dma_start(TG[p][0:L, :], bass.AP(t["kr_h"], g * (GRP * L), [[1, L], [1, GRP * L]])).then_inc(T_in[p], 16)

    def al_load(e, g, p):
        e.dma_start(EE[p][0:L, :], bass.AP(t["alS_h"], g * (GRP * N), [[0, L], [1, GRP * N]])).then_inc(A_in[p], 16)

    block = ctx.enter_context(nc.Block())

    @block.sync
    def _(e):
        for v, dst in ((a["logA"], natA), (a["Bp"], natB), (a["Cp"], natC)):
            e.dma_start(dst, v.rearrange("(h p) n -> p h n", p=P)).then_inc(coef_in, 16)
        for h in range(DH):
            e.dma_start(dtc[:, h:h + 1], a["log_dt"][h * P:(h + 1) * P].rearrange("(p o) -> p o", o=1)).then_inc(coef_in, 16)
        for u in range(2):
            e.dma_start(stage[:, u, :].rearrange("p (c k) -> p c k", c=4), w1v[u]).then_inc(w_in[u], 16)
        e.dma_start(context, a["ctx"].rearrange("b s d -> s b d")).then_inc(c_in, 16)
        for row, c in ((0, P), (N, 0)):
            e.dma_start(edit[row:row + 1, 0, c:c + P], a["Dp"][c:c + P].rearrange("(o d) -> o d", o=1)).then_inc(d_in, 16)
        for k in range(TILES // 4):
            e.dma_start(xres[:, 4 * k:4 * k + 4, :], xv[k]).then_inc(x_in, 16)
        e.wait_ge(coef, 4)
        e.dma_start(alS.rearrange("(h p) n -> p h n", p=P), al3[:, 0:DH, :]).then_inc(al_st, 16)
        for v, dst in ((a["gamma"], gam), (a["beta"], bet), (a["ab"], bo)):
            e.dma_start(dst[:, :], v.partition_broadcast(P)).then_inc(bc_in, 16)
        e.wait_ge(w_t, 1)
        e.dma_start(stage[:, 0, 0:512].rearrange("p (c k) -> p c k", c=2), awv).then_inc(w_in[0], 16)
        e.wait_ge(d_add, 4)
        e.dma_start(V[N:P, P:DM, :], V[0:N, 0:P, :]).then_inc(g_moved, 16)
        for v in range(2):
            e.wait_ge(w_t, v + 2)
            e.dma_start(stage[:, (1 + v) % 2, :], h1v[v]).then_inc(w_in[(1 + v) % 2], 16)
        with e.Fori(0, HC // 2 - 1) as k:
            for q in range(2):
                e.wait_ge(w_t, 2 * k + (q + 4))
                e.dma_start(stage[:, 1 - q, :], h1v[bass.ds(2 * k + (q + 2), 1)].rearrange("a p k -> (a p) k")).then_inc(w_in[1 - q], 16)
        w2v = a["w2"].rearrange("(u c p) k -> u p c k", c=4, p=P)
        e.wait_ge(c_t, 1)
        for u in range(2):
            e.dma_start(ahead_w2[u], w2v[u]).then_inc(ahead, 16)
        e.wait_ge(al_st, 16)
        for s in kr_st:
            e.wait_ge(s, 32)
        e.wait_ge(kr_pad, 16)
        for g in range(2):
            al_load(e, g, g)
            tg_load(e, g, g)
        with e.Fori(1, NGRP // 2) as it:
            for p in range(2):
                e.wait_ge(h_ps, 4 * it + (2 * p - 2))
                al_load(e, 2 * it + p, p)
                e.wait_ge(y_ps, 4 * it + (2 * p - 2))
                tg_load(e, 2 * it + p, p)
        for v, c0, n in ((a["s1"], 0, HC), (a["s2"], HC, HC), (a["hs1"], 2 * HC, HC), (a["hs2"], 3 * HC, HC), (a["s3"], 4 * HC, DH)):
            for c in range(n):
                e.dma_start(t["scl"][:, c0 + c:c0 + c + 1], v[c * P:(c + 1) * P].rearrange("(p o) -> p o", o=1)).then_inc(scl_in, 16)
        e.wait_ge(x1_rdy, 2)
        e.dma_start(t["x1t"][:, :].rearrange("p (j d) -> p j d", j=TPB), xres[:, 0:TPB, :]).then_inc(ahead, 16)
        with e.Fori(0, NBLK // 2) as it:
            for p in range(2):
                e.wait_ge(x1_rdy, 2 * it + (p + 2))
                e.dma_start(x1v[bass.ds(2 * it + p, 1)].rearrange("a p j d -> (a p) j d"),
                            xres[:, bass.ds(8 * it + 4 * p, 4), :]).then_inc(x1_st[p], 16)
        for s in x1_st:
            e.wait_ge(s, 16 * NBLK // 2)
        e.wait_ge(ahead, 48)
        e.wait_ge(scl_in, 16 * (4 * HC + DH))

    @block.gpsimd
    def _(e):
        e.memset(ident[:, :], 0.0).then_inc(const, 1)
        e.memset(rev[:, :], 0.0).then_inc(const, 1)
        e.memset(ones[:, :], 1.0).then_inc(const, 1)
        e.memset(mhalf[:, :], -0.5).then_inc(const, 1)
        e.iota(esc[:, :], [[0, 1]], base=-L, channel_multiplier=1, allow_small_or_imprecise_dtypes=True).then_inc(const, 1)
        e.wait_ge(const, 5)
        e.affine_select(out=ident[:, :], in_=ident[:, :], compare_op=ALU.not_equal, fill=1.0, base=0,
                        pattern=[[-1, P]], channel_multiplier=1).then_inc(const, 1)
        for h in range(2):
            blk = rev[64 * h:64 * h + 64, 64 * h:64 * h + 64]
            e.wait_ge(const, 6 + h)
            e.affine_select(out=blk, in_=blk, compare_op=ALU.not_equal, fill=1.0, base=-63,
                            pattern=[[1, 64]], channel_multiplier=1).then_inc(const, 1)
        e.wait_ge(const, 8)
        e.dma_start(kr[:, DM * L:DM * L + L], rev[0:1, L:2 * L]).then_inc(kr_pad, 16)
        e.wait_ge(coef_t, 1)
        e.wait_ge(al_st, 16)
        for p in range(2):
            e.memset(EE[p][N:P, :], 0.0).then_inc(ezero, 1)

        def inverse(g):
            e.wait_ge(var_rdy, 2 * g + 2)
            e.tensor_tensor(rs[:, :, bass.ds(4 * g, 4)], sv[:, :, bass.ds(4 * g, 4)], mhalf[:, :, :], ALU.pow).then_inc(powd, 1)

        def gamma(g):
            for j in range(4):
                e.wait_ge(z_rdy, 4 * g + (j + 1))
                e.tensor_tensor(zt[:, j, :], zt[:, j, :], gam[:, :], ALU.mult).then_inc(z_g, 1)
        e.wait_ge(ezero, 2)
        inverse(0)
        e.wait_ge(bc_in, 48)
        with e.Fori(0, TILES // 4 - 1) as g:
            inverse(g + 1)
            gamma(g)
        gamma(TILES // 4 - 1)

        def mask(p, turn):
            e.wait_ge(T_in[p], 16 * turn)
            e.sem_inc(step_g, 1)
            v = TG[p][0:L, :].rearrange("p (d t) -> p d t", d=GRP)
            e.affine_select(out=v, in_=v, compare_op=ALU.is_ge, fill=0.0, base=L - 1,
                            pattern=[[0, GRP], [-1, L]], channel_multiplier=-1).then_inc(t_mask, 1)
        with e.Fori(0, NGRP // 2) as it:
            for p in range(2):
                mask(p, it + 1)
        with e.Fori(0, NBLK // 2) as it:
            for p in range(2):
                e.wait_ge(zb_rdy, 8 * it + 4 * (p + 1))
                for j in range(4):
                    v = zb[p][:, j * DM:(j + 1) * DM]
                    e.tensor_tensor(v, v, bo[:, :], ALU.add).then_inc(zb_b, 1)

    @block.scalar
    def _(e):
        e.wait_ge(coef_in, 80)
        e.activation(dtc[:, 2:4], dtc[:, 0:2], ACT.Exp).then_inc(exps, 1)
        e.activation(natA, natA, ACT.Exp).then_inc(exps, 1)
        e.wait_ge(coef_t, 1)
        e.activation(a64[:, :], alT[0:N, :], ACT.Exp, scale=-float(L)).then_inc(pk_done, 1)
        for k in range(6):
            e.activation(pk[:, k, :], alT[:, P:DM], ACT.Exp, scale=-float(2 ** k)).then_inc(pk_done, 1)

        def w_evac(u, dst, src):
            e.wait_ge(w_t, u + 1)
            e.activation(dst, src, ACT.Copy).then_inc(w_ev, 1)
        for u in range(2):
            w_evac(u, t["w1T"][:, :, 512 * u:512 * u + 512].rearrange("p k (c o) -> p c k o", c=4),
                   wps[u][:, :].rearrange("p (c k o) -> p c k o", c=4, k=DH))
        e.wait_ge(c_t, 1)
        e.activation(t["keysT"][:, :], pair[1][:, 0:BATCH * DH * KEYS], ACT.Copy).then_inc(c_ev, 1)
        def h1_evac(v, q):
            w_evac(3 + v, t["h1T"][:, :, bass.ds(P * v, P)], wps[1 - q][:, :].rearrange("p (k o) -> p k o", k=HC))
        def norm_apply(g):
            e.wait_ge(nm_rdy, g + 1)
            for j in range(4):
                tile = 4 * g + j
                e.wait_ge(zt_free, tile + 1)
                e.activation(zt[:, j, :].unsqueeze(1), xres[:, bass.ds(tile, 1), :], ACT.Identity,
                             bias=ng[:, 1, bass.ds(tile, 1)], scale=rs[:, 1, bass.ds(tile, 1)]).then_inc(z_rdy, 1)
        def row_store(u):
            e.wait_ge(k_ev, u + 1)
            c = (u + 4) % 8 * 2048
            e.dma_start(kr[0, c:c + 2048].rearrange("(q m) -> q m", q=4), ksb[0:P:32, u % 4, :]).then_inc(kr_st[u % 4], 16)
        for u in range(8):
            e.wait_ge(k_ps, u + 1)
            if u >= 4:
                e.wait_ge(kr_st[u % 4], 16)
            e.activation(ksb[:, u % 4, :], kps[u % 2], ACT.Copy).then_inc(k_ev, 1)
            if u >= 1:
                row_store(u - 1)
            if u in (3, 6):
                norm_apply(u // 6)
        row_store(7)
        w_evac(2, woT[:, :, :].rearrange("p k (c o) -> p c k o", c=2), wps[0][:, 0:512].rearrange("p (c k o) -> p c k o", c=2, k=DH))
        for v in range(EARLY - 3):
            h1_evac(v, v % 2)
        with e.Fori(0, HC // 2 - 1) as k:
            for q in range(2):
                norm_apply(2 * k + (q + 2))
                h1_evac(2 * k + (q + 2), q)
        e.wait_ge(const, 8)
        e.wait_ge(g_moved, 16)
        e.wait_ge(g_row, 8)

        def decays(p, turn):
            e.wait_ge(A_in[p], 16 * turn)
            e.activation(EE[p][0:L, :], EE[p][0:L, :], ACT.Exp, scale=esc[:, :]).then_inc(e_rdy, 1)

        def entries(g, p):
            e.activation(TG[p][N:P, :], Vf[N:P, bass.ds(g * (GRP * L), GRP * L)], ACT.Copy).then_inc(g_cp, 1)

        def turns(it, half, last):
            for q in range(4):
                o = 4 * it + q
                e.wait_ge(y_ps, o + 1)
                e.activation(Vf[64 * half:64 * half + 64, bass.ds(o * 512 - half * (P * BC), 512)], yps[q % 2][0:L, :], ACT.Copy).then_inc(y_out, 1)
                if q % 2 == 0 and not last:
                    decays(q // 2, it + 2)
                elif not last:
                    entries(2 * it + (2 + q // 2), q // 2)
        for k in range(4):
            e.wait_ge(kr_st[k], 32)
        for p in range(2):
            decays(p, 1)
            entries(p, p)
        half_turns = NGRP // 4
        with e.Fori(0, half_turns) as it:
            turns(it, 0, False)
        with e.Fori(half_turns, 2 * half_turns - 1) as it:
            turns(it, 1, False)
        turns(2 * half_turns - 1, 1, True)
        with e.Fori(0, NBLK // 2) as it:
            for p in range(2):
                e.wait_ge(y_t, 2 * it + (p + 1))
                e.activation(yT[p].rearrange("p (h c t) -> p c h t", h=DH, c=8),
                             pair[p][:, :].rearrange("p (c h t) -> p c h t", c=8, h=DH), ACT.Copy).then_inc(y_tev, 1)
                for j in range(4):
                    tile = 8 * it + (4 * p + j)
                    if j == 0:
                        e.wait_ge(x1_rdy, 2 * it + p)
                    e.activation(zb[p][:, j * DM:(j + 1) * DM].unsqueeze(1), xres[:, bass.ds(tile, 1), :], ACT.Identity,
                                 bias=ng[:, 0, bass.ds(tile, 1)], scale=rs[:, 0, bass.ds(tile, 1)]).then_inc(zb_rdy, 1)

    @block.vector
    def _(e):
        e.wait_ge(exps, 2)
        for u, h in enumerate((0, 1, 0)):
            e.tensor_scalar(al3[:, u, :], natA[:, h, :], dtc[:, 2 + h:3 + h], None, ALU.mult).then_inc(coef, 1)
        e.tensor_tensor(natB, natB, natC, ALU.mult).then_inc(coef, 1)
        e.wait_ge(coef, 4)
        for u, h in enumerate((1, 0)):
            e.tensor_scalar(w10[:, u, :], natB[:, h, :], dtc[:, 2 + h:3 + h], None, ALU.mult).then_inc(coef, 1)
        e.wait_ge(coef_t, 1)
        e.tensor_copy(V[:, 0:P, L - 1:L], wT.unsqueeze(2)).then_inc(g_row, 1)
        e.tensor_copy(edit[N:N + 1, 1, 0:P], wT[N:N + 1, :]).then_inc(d_add, 1)
        e.tensor_copy(edit[N:N + 1, 1, P:DM], wT[0:1, :]).then_inc(d_add, 1)

        def double(k):
            n = 2 ** k
            e.wait_ge(pk_done, k + 2)
            e.wait_ge(g_row, k + 1)
            e.tensor_tensor(V[:, 0:P, L - 2 * n:L - n], V[:, 0:P, L - n:L],
                            pk[:, k, :].unsqueeze(2).to_broadcast([P, P, n]), ALU.mult).then_inc(g_row, 1)

        def to_chunks(g, j):
            if j == 0:
                e.wait_ge(k_ps, 4)
                e.wait_ge(g_moved, 16)
            e.wait_ge(z_g, 4 * g + (j + 1))
            e.tensor_tensor(V[0:L, :, bass.ds(8 * g + 2 * j, 1)], zt[0:64, j, :].unsqueeze(2), bet[0:64, :].unsqueeze(2), ALU.add)
            e.tensor_tensor(V[0:L, :, bass.ds(8 * g + (2 * j + 1), 1)], zt[64:P, j, :].unsqueeze(2), bet[64:P, :].unsqueeze(2), ALU.add).then_inc(zt_free, 1)

        def shifts(g, q):
            e.wait_ge(powd, g + 1)
            e.scalar_tensor_tensor(ng[:, :, bass.ds(4 * g, 4)], mv4[:, q, :, 0].unsqueeze(1).to_broadcast([P, 2, 4]), -1.0,
                                   rs[:, :, bass.ds(4 * g, 4)], ALU.mult, ALU.mult).then_inc(nm_rdy, 1)

        def stats(g, q, chunks=None):
            def between(*tiles):
                if chunks is not None:
                    for j in tiles:
                        to_chunks(chunks, j)
            e.wait_ge(aggr, 4 * g)
            for j in range(4):
                e.bn_stats(st[:, j, :], xres[:, bass.ds(4 * g + j, 1), :].rearrange("p a d -> p (a d)")).then_inc(stat, 1)
            between(0)
            if chunks is not None:
                shifts(chunks + 1, 1 - q)
            e.wait_ge(stat, 4 * g + 4)
            e.sem_inc(step_v, 1)
            for j in range(4):
                e.bn_aggr(mv4[:, q, j, :], st[:, j, :]).then_inc(aggr, 1)
            between(1)
            e.wait_ge(aggr, 4 * g + 4)
            here = bass.ds(4 * g, 4)
            e.tensor_scalar_add(sv[:, 0:1, here], mv4[:, q, :, 1].unsqueeze(1), EPS).then_inc(var_rdy, 1)
            between(2)
            e.wait_ge(var_rdy, 2 * g + 1)
            e.scalar_tensor_tensor(sv[:, 1:2, here], sv[:, 0:1, here], EPS, mv4[:, q, :, 1].unsqueeze(1), ALU.mult, ALU.add).then_inc(var_rdy, 1)

        for k in range(6):
            double(k)
        e.wait_ge(d_in, 32)
        e.wait_ge(d_add, 2)
        e.wait_ge(g_row, 7)
        for row, c in ((0, P), (N, 0)):
            v = V[row:row + 1, 0:P, L - 1]
            e.tensor_tensor(v, v, edit[row:row + 1, 0, c:c + P], ALU.add).then_inc(d_add, 1)
        e.wait_ge(x_in, 16 * TILES // 4)
        stats(0, 0)
        e.memset(zt[:, 0, 0:1], 0.0).then_inc(zt_free, 4)
        e.wait_ge(bc_in, 48)
        e.wait_ge(zt_free, 4)
        stats(1, 1)
        shifts(0, 0)
        with e.Fori(0, TILES // 8 - 1) as k:
            for q in range(2):
                stats(2 * k + (q + 2), q, 2 * k + q)
                to_chunks(2 * k + q, 3)
        shifts(7, 1)
        e.wait_ge(k_ps, 8)
        e.tensor_copy(V[N:N + 1, :, L - 1], edit[N:N + 1, 1, :]).then_inc(g_row, 1)
        e.wait_ge(c_ev, 1)
        for k in range(2):
            e.memset(hps[k][0:N, :], 0.0).then_inc(h_scan, 1)
        for g in (6, 7):
            for j in range(4):
                to_chunks(g, j)
        e.wait_ge(zt_free, TILES + 4)
        for k in range(2):
            e.memset(dec[0:N, k, :].rearrange("p (b c) -> p b c", c=CH)[:, :, 0], 0.0).then_inc(dec0, 1)
        e.wait_ge(dec0, 2)
        e.memset(dec[N:P, 0, 0:1], 0.0).then_inc(x1_rdy, 1)
        with e.Fori(0, DM // OCT // 4) as it:
            for q in range(4):
                o = 4 * it + q
                dv = dec[0:N, q % 2, :].rearrange("p (d b c) -> p d b c", d=OCT, b=BATCH)[:, :, :, 1:CH]
                e.wait_ge(h_scan, o + 1)
                e.tensor_copy(dv, a64[:, bass.ds(OCT * 4 * it + OCT * q, OCT)].unsqueeze(2).unsqueeze(3).to_broadcast([N, OCT, BATCH, CH - 1])).then_inc(dec_rdy, 1)
                e.wait_ge(dec_rdy, o + 1)
                e.wait_ge(h_ps, o + 1)
                if q % 2 == 0:
                    e.wait_ge(g_cp, 2 * it + (q // 2 + 1))
                e.tensor_tensor_scan(Vf[N:P, bass.ds(2048 * it + 512 * q, 512)], dec[0:N, q % 2, :], hps[q % 2][0:N, :], 0.0,
                                     ALU.mult, ALU.add).then_inc(h_scan, 1)
        with e.Fori(0, NBLK // 2) as it:
            for p in range(2):
                e.wait_ge(zb_b, 8 * it + 4 * (p + 1))
                e.wait_ge(pr_ps, 2 * it + (p + 1))
                e.tensor_tensor(zb[p], pair[2 + p][:, :], zb[p], ALU.add).then_inc(x1a, 1)
                e.wait_ge(x1a, 2 * it + (p + 1))
                v = xres[:, bass.ds(8 * it + 4 * p, 4), :].rearrange("p j d -> p (j d)")
                e.tensor_tensor(v, v, zb[p], ALU.add).then_inc(x1_rdy, 1)

    @block.tensor
    def _(e):
        e.wait_ge(const, 8)
        e.wait_ge(coef, 6)
        for h in range(DH):
            e.transpose(alT[:, h * P:(h + 1) * P], al3[:, h:h + 2, :].rearrange("p u n -> p (u n)"), ident[:, :])
        e.transpose(wT, w10[:, :, :].rearrange("p u n -> p (u n)"), ident[:, :]).then_inc(coef_t, 1)

        def w_transposes(u, ps, srcs):
            for n, src in enumerate(srcs):
                ins = e.transpose(ps[:, n * P:(n + 1) * P], src, ident[:, :])
            ins.then_inc(w_t, 1)
        def early_unit(u):
            e.wait_ge(w_in[u % 2], 16 * (u // 2 + 1))
            if u >= 2:
                e.wait_ge(w_ev, u - 1)
            w_transposes(u, wps[u % 2], [stage[:, u % 2, n * P:(n + 1) * P] for n in range(4 if u == 2 else 8)])
        for u in range(2):
            early_unit(u)
        e.wait_ge(c_in, 16)
        for b in range(BATCH):
            for h in range(DH):
                c = (DH * b + h) * KEYS
                ins = e.transpose(pair[1][:, c:c + KEYS], context[:, b, h * P:(h + 1) * P], ident[0:KEYS, 0:KEYS])
        ins.then_inc(c_t, 1)
        e.wait_ge(g_row, 7)
        e.wait_ge(d_add, 4)
        for u in range(8):
            if u >= 2:
                e.wait_ge(k_ev, u - 1)
            row = 0 if u < 4 else N
            for q in range(4):
                c = u % 4 * 32 + q * 8
                ins = e.matmul(kps[u % 2][32 * q:32 * q + 32, :], ones[row:row + N, 0:32], Vf[row:row + N, c * L:(c + 8) * L], start=True, stop=True)
            ins.then_inc(k_ps, 1)
        for u in range(2, EARLY):
            early_unit(u)

        with e.Fori(0, HC // 2 - 1) as k:
            for q in range(2):
                e.wait_ge(w_in[1 - q], 16 * k + 16 * (3 + q))
                e.wait_ge(w_ev, 2 * k + (q + 4))
                w_transposes(0, wps[1 - q], [stage[:, 1 - q, n * P:(n + 1) * P] for n in range(8)])
        e.wait_ge(zt_free, TILES + 4)
        e.wait_ge(ezero, 2)

        def states(o8, q, first_wait):
            e.wait_ge(*first_wait)
            for c in range(OCT):
                rhs = V4[:, bass.ds(o8 + c, 1), :, 0:CH - 1].rearrange("p a b c -> p (a b) c")
                out = hps[q % 2][0:N, c * BC:(c + 1) * BC].rearrange("p (b c) -> p b c", b=BATCH)[:, :, 1:CH]
                k = (q % 2) * OCT + c
                ins = e.matmul(out, EE[q // 2 % 2][:, k * N:(k + 1) * N], rhs, start=True, stop=True)
            ins.then_inc(h_ps, 1)

        def outputs(o8, q):
            e.sem_inc(step_t, 1)
            for c in range(OCT):
                k = (q % 2) * OCT + c
                rhs = V[:, bass.ds(o8 + c, 1), :].rearrange("p a c -> p (a c)")
                ins = e.matmul(yps[q % 2][0:L, c * BC:(c + 1) * BC], TG[q // 2][:, k * L:(k + 1) * L], rhs, start=True, stop=True)
            ins.then_inc(y_ps, 1)

        def turn(it, last):
            for q in range(4):
                if not (last and q == 3):
                    if q % 2 == 1:
                        e.wait_ge(e_rdy, 2 * it + ((q + 1) // 2 + 1))
                    states(32 * it + OCT * (q + 1), (q + 1) % 4, (h_scan, 4 * it + (q + 2)))
                if q % 2 == 0:
                    e.wait_ge(t_mask, 2 * it + (q // 2 + 1))
                    e.wait_ge(g_cp, 2 * it + (q // 2 + 1))
                e.wait_ge(h_scan, 4 * it + (q + 3))
                if not (isinstance(it, int) and 4 * it + q < 2):
                    e.wait_ge(y_out, 4 * it + (q - 1))
                outputs(32 * it + OCT * q, q)
        e.wait_ge(e_rdy, 1)
        states(0, 0, (h_scan, 1))
        turn(0, False)
        with e.Fori(1, DM // OCT // 4 - 1) as it:
            turn(it, False)
        turn(DM // OCT // 4 - 1, True)

        def y_transposes(i):
            if i >= 2:
                e.wait_ge(y_tev, i - 1)
            for c in range(8):
                ins = e.transpose(pair[i % 2][:, c * P:(c + 1) * P], V[:, 0:P, 8 * i + c], rev[:, :])
            ins.then_inc(y_t, 1)

        def project(i):
            e.wait_ge(y_tev, i + 1)
            if i >= 2:
                e.wait_ge(x1a, i - 1)
            for j in range(TPB):
                for h in range(DH):
                    ins = e.matmul(pair[2 + i % 2][:, j * DM:(j + 1) * DM], yT[i % 2][:, h * BLK + j * P:h * BLK + (j + 1) * P],
                                   woT[:, h, :], start=(h == 0), stop=(h == DH - 1))
            ins.then_inc(pr_ps, 1)
        e.wait_ge(w_ev, NW)
        e.wait_ge(y_out, DM // OCT)
        y_transposes(0)
        for i in range(NBLK):
            if i + 1 < NBLK:
                y_transposes(i + 1)
            project(i)


def attention_ffn_program(nc, ctx, a, t):
    def sb(name, shape, dt=F32):
        return ctx.enter_context(nc.sbuf_tensor(name, shape, dt))

    def sem(name):
        return ctx.enter_context(nc.semaphore(name))

    h1 = [sb("h1hi", [P, HC, BLK], F32R), sb("h1lo", [P, HC, BLK], F32R)]
    h2 = [sb("h2hi", [P, HC, BLK], F32R), sb("h2lo", [P, HC, BLK], F32R)]
    zT = [sb("zThi", [P, DH * BLK], F32R), sb("zTlo", [P, DH * BLK], F32R)]
    w2T = sb("w2T", [P, DH, HID], F32R)
    w3T = sb("w3T", [P, HC, DM], F32R)
    xr = sb("xr", [P, TPB * DM])
    nat = sb("nat", [P, TPB, DM])
    qa = sb("qa", [P, DH, BLK])
    prob = sb("prob", [P, 2, BLK])
    pT = sb("pT", [P, 4, BLK])
    kblk = sb("kblk", [P, 2 * BLK])
    vblk = sb("vblk", [P, DM])
    xwoT = sb("xwoT", [P, DH, DM])
    xbo = sb("xbo", [P, DM])
    hmask = sb("hmask", [P, 8])
    st = sb("st2", [P, TPB, 6])
    mv = sb("mv2", [P, TPB, 2])
    lnv = sb("lnv", [P, 3, TPB])
    ve, rs, mh = lnv[:, 0, :], lnv[:, 1, :], lnv[:, 2, :]
    red = sb("red", [P, 3, 2, 8])
    bits = sb("bits", [P, P], I32)
    most = sb("most", [P, 1], I32)
    warm = sb("warm", [P, 2])
    bit_row = bits[0:1, :]
    pair, ident, scl = t["pair"], t["ident"], t["scl"]
    x1d, x2d = t["x1d"], t["x2d"]
    w1T, h1T = t["w1T"], t["h1T"]
    keysT, x1t, vb, sg = (t[n] for n in ("keysT", "x1t", "vb", "sg"))
    h2T = sb("h2T", [P, HC, HID], F32R)
    stage = [vb[:, :, :].rearrange("p a t -> p (a t)"), sg[:, :, :].rearrange("p a t -> p (a t)")]
    t_ps = [pair[3][:, 512 * k:512 * (k + 1)] for k in range(2)]
    h_ps = [pair[k // 2][:, 512 * (k % 2):512 * (k % 2) + 512] for k in range(4)]
    sc1, sc2, sch, sc3 = scl[:, 0:8], scl[:, 8:16], (scl[:, 16:24], scl[:, 24:32]), scl[:, 32:34]

    w_in = [sem("pw_in0"), sem("pw_in1")]
    names = ("pw_t", "pw_ev", "xbo_in", "mk", "k_rdy", "values_rdy", "vb0",
             "stat2", "aggr2", "var_rdy", "rstd", "nat_rdy", "nat_t", "x1b", "sc_ps", "mx", "sub", "exped", "summed", "rcp", "p_rdy",
             "p_t", "t_ev", "av", "wo_ps", "x2_rdy", "z_hi", "z_lo", "mm", "sg_rdy", "v_rdy", "hi", "lo", "o_ev", "o_t", "fin",
             "x1_in", "v_in", "xr_in", "x2_st", "out_st", "step_v2", "step_s2", "raw_in", "checked", "folded", "col_st", "row_in", "flagged", "warm", "step_g2")
    S = {n: sem(n) for n in names}

    def blk_rows(d, i):
        return d.rearrange("(k j p) d -> k p j d", j=TPB, p=P)[bass.ds(i, 1)].rearrange("a p j d -> (a p) j d")

    w3v = a["w3"].rearrange("(u p) k -> u p k", p=P)
    h2v = a["h2"].rearrange("(u p) k -> u p k", p=P)
    xwv = a["xW"].rearrange("(c p) k -> p c k", p=P)
    NW = 5 + HC
    UNITS_AT = [2, 4, 6, 8, 10]

    raw_wide = [a[n].rearrange("(i p) k -> i p k", p=P) for n in ("h1", "h2")]
    raw_narrow = [a["w1"].rearrange("(i p) k -> i p k", p=P), a["w2"].rearrange("(i p) k -> i p k", p=P),
                  a["w3"].rearrange("(i r) (q k) -> i (r q) k", i=NBLK, q=4)]
    sg_flat = sg[:, :, :].rearrange("p a t -> p (a t)")
    CHECK = [10, 11, 12]

    TURN = [2, 5, 8, 11]
    SCORES_AT = [1, 3, 6]
    VALUES_AT = [6, 12]
    block = ctx.enter_context(nc.Block())

    @block.sync
    def _(e):
        def unit_load(u):
            dst = stage[u % 2]
            e.wait_ge(S["pw_t"], u - 1)
            if u == 2:
                e.dma_start(dst[:, 0:512].rearrange("p (c k) -> p c k", c=2), xwv).then_inc(w_in[u % 2], 16)
            else:
                e.dma_start(dst, w3v[u - 3] if u < 5 else h2v[u - 5]).then_inc(w_in[u % 2], 16)

        def attn_loads(j):
            if not (isinstance(j, int) and j == 0):
                e.wait_ge(S["x2_st"], 16 * j)
                e.sem_inc(S["step_s2"], 1)
                e.wait_ge(S["nat_rdy"], 8 * j)
                e.dma_start(x1t[:, :].rearrange("p (j d) -> p j d", j=TPB), blk_rows(x1d, j)).then_inc(S["x1_in"], 16)
            e.wait_ge(S["av"], 2 * j)
            seq = j // (T // BLK)
            for d in range(2):
                e.dma_start(vblk[KEYS * d:KEYS * (d + 1), :], a["ctx"][bass.ds(seq, 1)].rearrange("a s d -> (a s) d")).then_inc(S["v_in"], 16)

        def x2_store(j):
            e.wait_ge(S["x2_rdy"], j + 1)
            e.dma_start(blk_rows(x2d, j), x1t[:, :].rearrange("p (j d) -> p j d", j=TPB)).then_inc(S["x2_st"], 16)

        def res_load(i):
            e.wait_ge(S["x2_st"], 16 * i + 16)
            e.wait_ge(S["out_st"], 16 * i)
            e.dma_start(xr[:, :].rearrange("p (j d) -> p j d", j=TPB), blk_rows(x2d, i)).then_inc(S["xr_in"], 16)

        def raw_loads(i):
            for k, src in enumerate(raw_wide):
                e.wait_ge(*((S["v_rdy"], 8 * i + 8) if k == 0 else (S["checked"], 12 * i + 5)))
                e.dma_start(sg_flat, src[bass.ds(i, 1)].rearrange("a p k -> (a p) k")).then_inc(S["raw_in"], 16)
            e.wait_ge(S["checked"], 12 * i + 9)
            for k, src in enumerate(raw_narrow):
                e.dma_start(sg_flat[:, k * DM:(k + 1) * DM], src[bass.ds(i, 1)].rearrange("a p k -> (a p) k")).then_inc(S["raw_in"], 16)

        def out_store(i):
            e.wait_ge(S["fin"], i + 1)
            e.dma_start(blk_rows(a["out"].rearrange("b t d -> (b t) d"), i), xr[:, :].rearrange("p (j d) -> p j d", j=TPB)).then_inc(S["out_st"], 16)
        attn_loads(0)
        e.dma_start(xbo[:, :], a["xb"].partition_broadcast(P)).then_inc(S["xbo_in"], 16)
        for u in range(2, NW):
            unit_load(u)
        x2_store(0)
        attn_loads(1)
        with e.Fori(0, NBLK - 2) as i:
            res_load(i)
            raw_loads(i)
            x2_store(i + 1)
            attn_loads(i + 2)
            out_store(i)
        res_load(NBLK - 2)
        raw_loads(NBLK - 2)
        x2_store(NBLK - 1)
        out_store(NBLK - 2)
        res_load(NBLK - 1)
        raw_loads(NBLK - 1)
        e.wait_ge(S["folded"], 2)
        e.dma_start(t["flag_col"], most[:, :]).then_inc(S["col_st"], 16)
        e.wait_ge(S["col_st"], 16)
        e.dma_start(bit_row, t["flag_col"].rearrange("p o -> o p")).then_inc(S["row_in"], 16)
        out_store(NBLK - 1)
        e.wait_ge(S["out_st"], 16 * NBLK)

    @block.gpsimd
    def _(e):
        e.memset(hmask[:, :], 1.0).then_inc(S["mk"], 1)
        e.memset(mh, -0.5).then_inc(S["mk"], 1)
        e.wait_ge(S["mk"], 2)
        e.affine_select(out=hmask[:, :], in_=hmask[:, :], compare_op=ALU.is_ge, fill=0.0, base=0, pattern=[[-HD, 8]], channel_multiplier=1).then_inc(S["mk"], 1)
        e.wait_ge(S["mk"], 3)
        e.affine_select(out=hmask[:, :], in_=hmask[:, :], compare_op=ALU.is_ge, fill=0.0, base=HD - 1, pattern=[[HD, 8]], channel_multiplier=-1).then_inc(S["mk"], 1)
        e.wait_ge(S["mk"], 4)

        def rstd(n):
            e.wait_ge(S["var_rdy"], n + 1)
            e.tensor_tensor(rs, ve, mh, ALU.pow).then_inc(S["rstd"], 1)

        def out_bias(j):
            e.wait_ge(S["nat_rdy"], 8 * j + 4)
            for m in range(TPB):
                v = x1t[:, m * DM:(m + 1) * DM]
                e.tensor_tensor(v, v, xbo[:, :], ALU.add).then_inc(S["x1b"], 1)

        def keys(j):
            e.wait_ge(S["sc_ps"], 4 * j)
            for h in range(DH):
                src = keysT[:, bass.ds(j % NBLK // (T // BLK) * (DH * KEYS) + h * KEYS, KEYS)].unsqueeze(1).to_broadcast([P, 8, KEYS])
                e.tensor_tensor(kblk[:, h * BLK:(h + 1) * BLK].rearrange("p (g k) -> p g k", g=8), src,
                                hmask[:, :].unsqueeze(2).to_broadcast([P, 8, KEYS]), ALU.mult).then_inc(S["k_rdy"], 1)

        def values_clear(j):
            e.wait_ge(S["v_in"], 32 * j + 32)
            for d in range(2):
                e.wait_ge(S["values_rdy"], 2 * j + d)
                e.sem_inc(S["step_g2"], 1)
                heads = vblk[KEYS * d:KEYS * (d + 1), :].rearrange("p (r g d) -> p r g d", g=2, d=HD)
                e.memset(heads[:, :, 1 - d, :], 0.0).then_inc(S["values_rdy"], 1)
            e.wait_ge(S["values_rdy"], 2 * j + 2)

        def body(i, attn):
            if attn:
                rstd(2 * i + 2)
            for m in range(HC - 2):
                e.wait_ge(S["hi"], 24 * i + (m + 1))
                e.tensor_tensor(h1[1][:, m, :], vb[:, m % 2, :], h1[0][:, m, :], ALU.subtract).then_inc(S["lo"], 1)
            if attn:
                values_clear(i + 1)
                out_bias(i + 1)
                keys(i + 2)
                rstd(2 * i + 3)
        rstd(0)
        keys(0)
        values_clear(0)
        e.wait_ge(S["xbo_in"], 16)
        out_bias(0)
        keys(1)
        rstd(1)
        with e.Fori(0, NBLK - 1) as i:
            body(i, True)
        body(NBLK - 1, False)

    @block.scalar
    def _(e):
        def w_evac(u, dst, src):
            e.wait_ge(S["pw_t"], u + 1)
            e.activation(dst, src, ACT.Copy).then_inc(S["pw_ev"], 1)

        def unit_evac(u):
            src = pair[u % 2][:, :]
            if u < 2:
                w_evac(u, w2T[:, :, 512 * u:512 * u + 512].rearrange("p k (c o) -> p c k o", c=4), src.rearrange("p (c k o) -> p c k o", c=4, k=DH))
            elif u > 2:
                dst = w3T[:, :, P * (u - 3):P * (u - 2)] if u < 5 else h2T[:, :, P * (u - 5):P * (u - 4)]
                w_evac(u, dst, src.rearrange("p (k o) -> p k o", k=HC))
            else:
                w_evac(u, xwoT[:, :, :].rearrange("p k (c o) -> p c k o", c=2), src[:, 0:512].rearrange("p (c k o) -> p c k o", c=2, k=DH))

        def table(function, n):
            e.wait_ge(S["warm"], n)
            e.activation(warm[:, 1:2], warm[:, 0:1], function).then_inc(S["warm"], 1)

        def q_evac(j):
            e.wait_ge(S["nat_t"], 2 * j + 1)
            e.activation(qa[:, :, :].rearrange("p a t -> p (a t)"), pair[3][:, :], ACT.Copy).then_inc(S["t_ev"], 1)

        def exp(j, u, n):
            table(ACT.Exp, n)
            e.wait_ge(S["sub"], 4 * j + (u + 1))
            e.activation(prob[:, :, :], prob[:, :, :], ACT.Exp, scale=HD ** -0.5).then_inc(S["exped"], 1)

        def turn_evac(j, u):
            e.wait_ge(S["p_t"], 4 * j + (u + 1))
            first = u % 2 * 2 * P
            if u % 2 == 0:
                e.wait_ge(S["av"], 2 * j + u // 2)
            e.activation(pT[:, :, first:first + 2 * P].rearrange("p r (b t) -> p b r t", b=2),
                         pair[3][:, :].rearrange("p (b r t) -> p b r t", b=2, r=4), ACT.Copy).then_inc(S["t_ev"], 1)

        def av_evac(j, h):
            e.wait_ge(S["av"], 2 * j + (h + 1))
            e.activation(qa[:, h, :], t_ps[h], ACT.Copy).then_inc(S["t_ev"], 1)

        def z_evac(j):
            e.wait_ge(S["nat_t"], 2 * j + 2)
            e.activation(zT[0][:, :], pair[3][:, :], ACT.Copy).then_inc(S["z_hi"], 1)

        def gated(i, attn):
            for m in range(HC + 1):
                if attn and m == 5:
                    q_evac(i + 1)
                if m < HC:
                    e.wait_ge(S["mm"], 26 * i + (m + 1))
                    e.wait_ge(S["v_rdy"], 8 * i + max(m - 1, 0))
                    e.activation(sg[:, m % 2, :], pair[m % 2][:, 0:512], ACT.Silu, scale=sc1[:, m:m + 1]).then_inc(S["sg_rdy"], 1)
                if m > 0:
                    e.wait_ge(S["v_rdy"], 8 * i + m)
                    e.activation(h1[0][:, m - 1, :], vb[:, (m - 1) % 2, :], ACT.Copy).then_inc(S["hi"], 1)

        def hidden(i, s):
            dst = h2 if s < HC else h1
            m = s % HC
            sc = sch[s // HC][:, m:m + 1]
            e.wait_ge(S["mm"], 26 * i + (HC + s + 1))
            e.wait_ge(S["lo"], 24 * i + (HC + s - 1))
            e.activation(vb[:, s % 2, :], h_ps[s % 4], ACT.Gelu, scale=sc)
            e.activation(dst[0][:, m, :], h_ps[s % 4], ACT.Gelu, scale=sc).then_inc(S["hi"], 1)

        def out_evac(i, m):
            e.wait_ge(S["mm"], 26 * i + (25 + m))
            e.wait_ge(S["checked"], 12 * i + 13)
            e.activation(sg[:, m, :], h_ps[m], ACT.Copy, scale=sc3[:, m:m + 1]).then_inc(S["o_ev"], 1)

        def body(i, attn):
            j = i + 1
            turns = 9 * i + 4
            table(ACT.Silu, turns)
            gated(i, attn)
            if attn:
                exp(j, 0, turns + 1)
            table(ACT.Gelu, turns + (2 if attn else 1))
            for s in range(2 * HC):
                hidden(i, s)
                if attn and s in TURN:
                    u = TURN.index(s)
                    turn_evac(j, u)
                    if u < 3:
                        exp(j, u + 1, turns + (2 * u + 3))
                        table(ACT.Gelu, turns + (2 * u + 4))
                if attn and s in VALUES_AT:
                    av_evac(j, VALUES_AT.index(s))
            out_evac(i, 0)
            if attn:
                z_evac(j)
            out_evac(i, 1)
        for u in range(UNITS_AT[0]):
            unit_evac(u)
        q_evac(0)
        e.wait_ge(S["vb0"], 1)
        for u in range(4):
            exp(0, u, u)
            unit_evac(UNITS_AT[u])
            if u == 2:
                av_evac(0, 0)
            for w in range(UNITS_AT[u] + 1, UNITS_AT[u + 1]):
                unit_evac(w)
            turn_evac(0, u)
        av_evac(0, 1)
        for w in range(UNITS_AT[4], NW):
            unit_evac(w)
        z_evac(0)
        with e.Fori(0, NBLK - 1) as i:
            body(i, True)
        body(NBLK - 1, False)

    @block.vector
    def _(e):
        e.memset(bits[:, :], 0).then_inc(S["checked"], 1)
        e.memset(warm[:, :], 0.0).then_inc(S["vb0"], 1)

        def stats(n):
            for m in range(TPB):
                e.bn_stats(st[:, m, :], x1t[:, m * DM:(m + 1) * DM]).then_inc(S["stat2"], 1)
            e.wait_ge(S["stat2"], 4 * n + 4)
            e.wait_ge(S["nat_rdy"], 4 * n)
            e.sem_inc(S["step_v2"], 1)
            for m in range(TPB):
                e.bn_aggr(mv[:, m, :], st[:, m, :]).then_inc(S["aggr2"], 1)
            e.wait_ge(S["aggr2"], 4 * n + 4)
            e.tensor_scalar_add(ve, mv[:, :, 1], EPS).then_inc(S["var_rdy"], 1)

        def normed(n):
            e.wait_ge(S["rstd"], n + 1)
            e.wait_ge(S["nat_t"], n)
            for m in range(TPB):
                e.tensor_scalar(nat[:, m, :], x1t[:, m * DM:(m + 1) * DM], mv[:, m, 0:1], rs[:, m:m + 1], ALU.subtract, ALU.mult).then_inc(S["nat_rdy"], 1)

        def pairwise(v):
            return v.rearrange("p b (h k) -> p b h k", h=8)
        s4 = pair[2][:, :].rearrange("p (b h k) -> p b h k", b=2, h=8)
        p4 = pairwise(prob[:, :, :])

        def spread(k):
            return red[:, k, :, :].unsqueeze(3).to_broadcast([P, 2, 8, KEYS])

        def maxima(j, u):
            e.wait_ge(S["sc_ps"], 4 * j + (u + 1))
            e.tensor_reduce(red[:, 0, :, :], s4, AX.X, ALU.max).then_inc(S["mx"], 1)

        def shifted(j, u):
            e.wait_ge(S["mx"], 4 * j + (u + 1))
            if u > 0:
                e.wait_ge(S["p_t"], 4 * j + u)
            e.tensor_tensor(p4, s4, spread(0), ALU.subtract).then_inc(S["sub"], 1)

        def normalised(j, u):
            e.wait_ge(S["exped"], 4 * j + (u + 1))
            e.tensor_reduce(red[:, 1, :, :], p4, AX.X, ALU.add).then_inc(S["summed"], 1)
            e.wait_ge(S["summed"], 4 * j + (u + 1))
            e.reciprocal(red[:, 2, :, :], red[:, 1, :, :]).then_inc(S["rcp"], 1)
            e.wait_ge(S["rcp"], 4 * j + (u + 1))
            e.tensor_tensor(p4, p4, spread(2), ALU.mult).then_inc(S["p_rdy"], 1)

        def residual(j):
            e.wait_ge(S["wo_ps"], j + 1)
            e.wait_ge(S["x1b"], 4 * j + 4)
            e.tensor_tensor(x1t[:, :], pair[3][:, :], x1t[:, :], ALU.add).then_inc(S["x2_rdy"], 1)
            e.wait_ge(S["x2_rdy"], j + 1)

        def z_lo(j):
            e.wait_ge(S["z_hi"], j + 1)
            e.tensor_tensor(zT[1][:, :], pair[3][:, :], zT[0][:, :], ALU.subtract).then_inc(S["z_lo"], 1)

        def low(i, n, dst):
            e.wait_ge(S["hi"], 24 * i + (n + 1))
            e.tensor_tensor(dst[1][:, n % HC, :], vb[:, n % 2, :], dst[0][:, n % HC, :], ALU.subtract).then_inc(S["lo"], 1)

        def checked(i, k):
            e.wait_ge(S["raw_in"], 80 * i + (16, 32, 80)[k])
            raw = sg_flat.bitcast(I32)
            folds = ((0, 512, 512), (0, 256, 256), (0, P, P)) if k < 2 else ((0, DM, DM), (0, 2 * DM, DM), (0, P, P))
            for n, (to, other, width) in enumerate(folds):
                e.wait_ge(S["checked"], 12 * i + (4 * k + n + 1))
                e.tensor_tensor(raw[:, to:to + width], raw[:, to:to + width], raw[:, other:other + width], ALU.bitwise_or).then_inc(S["checked"], 1)
            e.wait_ge(S["checked"], 12 * i + (4 * k + 4))
            e.tensor_tensor(bits[:, :], bits[:, :], raw[:, 0:P], ALU.bitwise_or).then_inc(S["checked"], 1)

        def body(i, attn):
            j = i + 1
            if attn:
                e.wait_ge(S["x1_in"], 16 * j)
                stats(2 * j)
            for m in range(HC):
                e.wait_ge(S["sg_rdy"], 8 * i + (m + 1))
                e.wait_ge(S["lo"], 24 * i + max(m - 1, 0))
                e.scalar_tensor_tensor(vb[:, m % 2, :], pair[m % 2][:, 512:1024], sc2[:, m:m + 1], sg[:, m % 2, :],
                                       ALU.mult, ALU.mult).then_inc(S["v_rdy"], 1)
                if m == HC - 1:
                    e.wait_ge(S["lo"], 24 * i + m - 1)
                    low(i, m - 1, h1)
                    low(i, m, h1)
                if attn and m == 1:
                    normed(2 * j)
            if attn:
                maxima(j, 0)
                shifted(j, 0)
            for s in range(2 * HC):
                low(i, HC + s, h2 if s < HC else h1)
                if attn and s in TURN and s != TURN[3]:
                    shifted(j, TURN.index(s) + 1)
                if attn and s + 1 in TURN and s + 1 != TURN[3]:
                    maxima(j, TURN.index(s + 1) + 1)
                if attn and s + 2 in TURN:
                    normalised(j, TURN.index(s + 2))
                if attn and s == 13:
                    residual(j)
                    stats(2 * j + 1)
                if attn and s == 14:
                    normed(2 * j + 1)
                if s in CHECK:
                    checked(i, CHECK.index(s))
            if attn:
                z_lo(j)
            else:
                e.wait_ge(S["checked"], 12 * NBLK + 1)
                e.tensor_scalar(bits[:, :], bits[:, :], 0xFFF, None, ALU.bitwise_and).then_inc(S["folded"], 1)
                e.wait_ge(S["folded"], 1)
                e.tensor_reduce(most[:, :], bits[:, :], AX.X, ALU.max).then_inc(S["folded"], 1)
                e.wait_ge(S["row_in"], 16)
                e.tensor_reduce(t["flag"][:, :], bit_row, AX.X, ALU.max).then_inc(S["flagged"], 1)
            e.wait_ge(S["o_t"], i + 1)
            e.wait_ge(S["xr_in"], 16 * i + 16)
            e.tensor_tensor(xr[:, :], pair[2][:, :], xr[:, :], ALU.add).then_inc(S["fin"], 1)
        stats(0)
        normed(0)
        maxima(0, 0)
        for u in range(4):
            shifted(0, u)
            normalised(0, u)
            if u < 3:
                maxima(0, u + 1)
        residual(0)
        stats(1)
        normed(1)
        z_lo(0)
        with e.Fori(0, NBLK - 1) as i:
            body(i, True)
        body(NBLK - 1, False)

    @block.tensor
    def _(e):
        def unit_turn(u):
            if u >= 2:
                e.wait_ge(w_in[u % 2], 16 * (u // 2))
                e.wait_ge(S["pw_ev"], u - 1)
            for n in range(HC if u != 2 else 4):
                ins = e.transpose(pair[u % 2][:, n * P:(n + 1) * P], stage[u % 2][:, n * P:(n + 1) * P], ident[:, :])
            ins.then_inc(S["pw_t"], 1)

        def turn_nat(n):
            e.wait_ge(S["nat_rdy"], 4 * n + 4)
            for k in range(DH):
                for m in range(TPB):
                    ins = e.transpose(pair[3][:, k * BLK + m * P:k * BLK + (m + 1) * P], nat[:, m, k * P:(k + 1) * P], ident[:, :])
            ins.then_inc(S["nat_t"], 1)

        def turn_q(j):
            e.wait_ge(S["z_lo"], j)
            turn_nat(2 * j)

        def turn_z(j):
            e.wait_ge(S["x2_rdy"], j + 1)
            turn_nat(2 * j + 1)

        def scores(j, u):
            if u == 0:
                e.wait_ge(S["t_ev"], 7 * j + 1)
                e.wait_ge(S["k_rdy"], 2 * j + 2)
                if not isinstance(j, int):
                    e.wait_ge(S["fin"], j - 1)
            else:
                e.wait_ge(S["sub"], 4 * j + u)
            h = u // 2
            for b in range(2):
                tile = 2 * (u % 2) + b
                ins = e.matmul(pair[2][:, b * BLK:(b + 1) * BLK], qa[:, h, tile * P:(tile + 1) * P], kblk[:, h * BLK:(h + 1) * BLK], start=True, stop=True)
            ins.then_inc(S["sc_ps"], 1)

        def turn_p(j, u):
            e.wait_ge(S["p_rdy"], 4 * j + (u + 1))
            e.wait_ge(S["t_ev"], 7 * j + (1 + u + u // 2))
            for b in range(2):
                for r in range(4):
                    ins = e.transpose(pair[3][:, b * BLK + r * P:b * BLK + (r + 1) * P], prob[:, b, r * P:(r + 1) * P], ident[:, :])
            ins.then_inc(S["p_t"], 1)

        def values(j, h):
            if h == 0:
                e.wait_ge(S["values_rdy"], 2 * j + 2)
            e.wait_ge(S["t_ev"], 7 * j + (3 if h == 0 else 6))
            for r in range(4):
                c = (4 * h + r) * 32
                ins = e.matmul(t_ps[h][32 * r:32 * r + 32, :], vblk[:, c:c + 32], pT[:, r, :], start=True, stop=True)
            ins.then_inc(S["av"], 1)

        def project(j):
            e.wait_ge(S["t_ev"], 7 * j + 7)
            for m in range(TPB):
                for k in range(DH):
                    ins = e.matmul(pair[3][:, m * DM:(m + 1) * DM], qa[:, k, m * P:(m + 1) * P], xwoT[:, k, :], start=(k == 0), stop=(k == DH - 1))
            ins.then_inc(S["wo_ps"], 1)

        def gated(i, m):
            if m == 0:
                e.wait_ge(S["z_lo"], i + 1)
                e.wait_ge(S["o_ev"], 2 * i)
            elif m >= 2:
                e.wait_ge(S["v_rdy"], 8 * i + (m - 1))
            for g, w in enumerate((w1T, w2T)):
                for k in range(DH):
                    for part in range(2):
                        ins = e.matmul(pair[m % 2][:, 512 * g:512 * g + 512], w[:, k, m * P:(m + 1) * P], zT[part][:, k * BLK:(k + 1) * BLK],
                                       start=(k == 0 and part == 0), stop=(k == DH - 1 and part == 1))
            ins.then_inc(S["mm"], 1)

        def product(i, s, w, src, bank):
            m = s % HC
            for k in range(HC):
                if m == 0:
                    e.wait_ge(S["lo"], 24 * i + (HC * (s // HC) + k + 1))
                for part in range(2):
                    ins = e.matmul(bank, w[:, k, m * P:(m + 1) * P], src[part][:, k, :],
                                   start=(k == 0 and part == 0), stop=(k == HC - 1 and part == 1))
            ins.then_inc(S["mm"], 1)

        def hidden(i, s):
            if s < 2:
                e.wait_ge(S["v_rdy"], 8 * i + 7)
            elif s < 4:
                e.wait_ge(S["v_rdy"], 8 * i + 8)
            else:
                e.wait_ge(S["hi"], 24 * i + (HC + s - 3))
            product(i, s, h1T if s < HC else h2T, h1 if s < HC else h2, h_ps[s % 4])

        def last(i, m):
            e.wait_ge(S["hi"], 24 * i + (21 + m))
            product(i, 16 + m, w3T, h1, h_ps[m])

        def turn_out(i):
            for k in range(DH):
                e.wait_ge(S["o_ev"], 2 * i + (k + 1))
                for m in range(TPB):
                    ins = e.transpose(pair[2][:, m * DM + k * P:m * DM + (k + 1) * P], sg[:, k, m * P:(m + 1) * P], ident[:, :])
            ins.then_inc(S["o_t"], 1)

        def body(i, attn):
            j = i + 1
            for m in range(HC):
                gated(i, m)
                if attn and m == 3:
                    turn_q(j)
                if attn and m == 6:
                    scores(j, 0)
            for s in range(2 * HC):
                hidden(i, s)
                if attn and s in TURN:
                    turn_p(j, TURN.index(s))
                if attn and s in SCORES_AT:
                    scores(j, SCORES_AT.index(s) + 1)
                if attn and s in VALUES_AT:
                    values(j, VALUES_AT.index(s))
                if attn and s == 13:
                    project(j)
            last(i, 0)
            if attn:
                turn_z(j)
            last(i, 1)
            turn_out(i)
        for u in range(UNITS_AT[0]):
            unit_turn(u)
        turn_q(0)
        scores(0, 0)
        for u in range(4):
            unit_turn(UNITS_AT[u])
            if u == 2:
                values(0, 0)
            if u < 3:
                scores(0, u + 1)
            for w in range(UNITS_AT[u] + 1, UNITS_AT[u + 1]):
                unit_turn(w)
            turn_p(0, u)
        values(0, 1)
        e.wait_ge(S["pw_ev"], 3)
        project(0)
        for w in range(UNITS_AT[4], NW):
            unit_turn(w)
        turn_z(0)
        e.wait_ge(S["pw_ev"], NW)
        with e.Fori(0, NBLK - 1) as i:
            body(i, True)
        body(NBLK - 1, False)


def exact_weights_program(nc, ctx, a, t):
    def sb(name, shape, dt=F32):
        return ctx.enter_context(nc.sbuf_tensor(name, shape, dt))

    def sem(name):
        return ctx.enter_context(nc.semaphore(name))

    turned = {"w1": sb("w1X", [P, DH, HID]), "w2": sb("w2X", [P, DH, HID]), "w3": sb("w3X", [P, HC, DM]),
              "h1": sb("h1X", [P, HC, HID]), "h2": sb("h2X", [P, HC, HID])}
    stage = [sb("stageX0", [P, 1024]), sb("stageX1", [P, 1024])]
    ha = sb("haX", [P, HC, BLK])
    hb = sb("hbX", [P, HC, BLK])
    zT = sb("zTX", [P, DH * BLK])
    xt = sb("xtX", [P, TPB * DM])
    nat = sb("natX", [P, TPB, DM])
    sg = sb("sgX", [P, 2, BLK])
    st = sb("stX", [P, TPB, 6])
    mv = sb("mvX", [P, TPB, 2])
    lnv = sb("lnvX", [P, 3, TPB])
    ve, rs, mh = lnv[:, 0, :], lnv[:, 1, :], lnv[:, 2, :]
    pair, ident, scl = t["pair"], t["ident"], t["scl"]
    h_ps = [pair[k // 2][:, 512 * (k % 2):512 * (k % 2) + 512] for k in range(4)]
    sc1, sc2, sch, sc3 = scl[:, 0:8], scl[:, 8:16], (scl[:, 16:24], scl[:, 24:32]), scl[:, 32:34]
    w_in = [sem("xw_in0"), sem("xw_in1")]
    w_t, w_ev, x_in, half, stat, aggr, var_rdy, rstd, nat_rdy, nat_t, z_rdy = (sem("x" + n) for n in (
        "w_t", "w_ev", "x_in", "half", "stat", "aggr", "var_rdy", "rstd", "nat_rdy", "nat_t", "z_rdy"))
    mm, sg_rdy, gate_rdy, act_rdy, o_ev, o_t, fin, out_st, step_v = (sem("x" + n) for n in (
        "mm", "sg_rdy", "gate_rdy", "act_rdy", "o_ev", "o_t", "fin", "out_st", "step_v"))

    def rows(d, i):
        return d.rearrange("(k j p) d -> k p j d", j=TPB, p=P)[bass.ds(i, 1)].rearrange("a p j d -> (a p) j d")
    xt3 = xt[:, :].rearrange("p (j d) -> p j d", j=TPB)
    natural = {n: a[n].rearrange("(u c p) k -> u p c k", c=4, p=P) for n in ("w1", "w2")}
    natural.update({n: a[n].rearrange("(u p) k -> u p k", p=P) for n in ("w3", "h1", "h2")})
    NARROW, WIDE = (("w1", 0), ("w2", 2), ("w3", 4)), (("h1", 6), ("h2", 6 + HC))

    block = ctx.enter_context(nc.Block())

    def needed(e):
        return e.value_load(t["flag"][0:1, 0:1], min_val=0, max_val=0xFFF) > 0

    @block.sync
    def _(e):
        with e.If(needed(e)):
            for n, base in NARROW:
                for u in range(2):
                    if base > 0:
                        e.wait_ge(w_t, base + u - 1)
                    dst = stage[u][:, :].rearrange("p (c k) -> p c k", c=4) if n != "w3" else stage[u][:, :]
                    e.dma_start(dst, natural[n][u]).then_inc(w_in[u], 16)
            for n, base in WIDE:
                with e.Fori(0, HC // 2) as k:
                    for q in range(2):
                        e.wait_ge(w_t, 2 * k + (base + q - 1))
                        e.dma_start(stage[q][:, :], natural[n][bass.ds(2 * k + q, 1)].rearrange("a p k -> (a p) k")).then_inc(w_in[q], 16)
            with e.Fori(0, NBLK) as i:
                e.wait_ge(out_st, 16 * i)
                e.dma_start(xt3, rows(t["x2d"], i)).then_inc(x_in, 16)
                e.wait_ge(fin, i + 1)
                e.dma_start(rows(a["out"].rearrange("b t d -> (b t) d"), i), xt3).then_inc(out_st, 16)
            e.wait_ge(out_st, 16 * NBLK)

    @block.gpsimd
    def _(e):
        with e.If(needed(e)):
            e.memset(mh, -0.5).then_inc(half, 1)
            e.wait_ge(half, 1)
            with e.Fori(0, NBLK) as i:
                e.wait_ge(var_rdy, i + 1)
                e.tensor_tensor(rs, ve, mh, ALU.pow).then_inc(rstd, 1)

    @block.scalar
    def _(e):
        with e.If(needed(e)):
            for n, base in NARROW:
                for u in range(2):
                    e.wait_ge(w_t, base + u + 1)
                    if n == "w3":
                        e.activation(turned[n][:, :, P * u:P * (u + 1)], pair[u][:, :].rearrange("p (k o) -> p k o", k=HC), ACT.Copy).then_inc(w_ev, 1)
                    else:
                        e.activation(turned[n][:, :, 512 * u:512 * u + 512].rearrange("p k (c o) -> p c k o", c=4),
                                     pair[u][:, :].rearrange("p (c k o) -> p c k o", c=4, k=DH), ACT.Copy).then_inc(w_ev, 1)
            for n, base in WIDE:
                with e.Fori(0, HC // 2) as k:
                    for q in range(2):
                        e.wait_ge(w_t, 2 * k + (base + q + 1))
                        e.activation(turned[n][:, :, bass.ds(2 * P * k + P * q, P)], pair[q][:, :].rearrange("p (k o) -> p k o", k=HC), ACT.Copy).then_inc(w_ev, 1)
            with e.Fori(0, NBLK) as i:
                e.wait_ge(nat_t, i + 1)
                e.activation(zT[:, :], pair[3][:, :], ACT.Copy).then_inc(z_rdy, 1)
                for m in range(HC):
                    e.wait_ge(mm, 26 * i + (m + 1))
                    e.wait_ge(gate_rdy, 8 * i + max(m - 1, 0))
                    e.activation(sg[:, m % 2, :], pair[m % 2][:, 0:512], ACT.Silu, scale=sc1[:, m:m + 1]).then_inc(sg_rdy, 1)
                for s in range(2 * HC):
                    m = s % HC
                    e.wait_ge(mm, 26 * i + (HC + s + 1))
                    e.activation((hb if s < HC else ha)[:, m, :], h_ps[s % 4], ACT.Gelu, scale=sch[s // HC][:, m:m + 1]).then_inc(act_rdy, 1)
                for m in range(DH):
                    e.wait_ge(mm, 26 * i + (25 + m))
                    e.activation(sg[:, m, :], h_ps[m], ACT.Copy, scale=sc3[:, m:m + 1]).then_inc(o_ev, 1)

    @block.vector
    def _(e):
        with e.If(needed(e)):
            with e.Fori(0, NBLK) as i:
                e.wait_ge(x_in, 16 * i + 16)
                for m in range(TPB):
                    e.bn_stats(st[:, m, :], xt[:, m * DM:(m + 1) * DM]).then_inc(stat, 1)
                e.wait_ge(stat, 4 * i + 4)
                e.sem_inc(step_v, 1)
                for m in range(TPB):
                    e.bn_aggr(mv[:, m, :], st[:, m, :]).then_inc(aggr, 1)
                e.wait_ge(aggr, 4 * i + 4)
                e.tensor_scalar_add(ve, mv[:, :, 1], EPS).then_inc(var_rdy, 1)
                e.wait_ge(rstd, i + 1)
                for m in range(TPB):
                    e.tensor_scalar(nat[:, m, :], xt[:, m * DM:(m + 1) * DM], mv[:, m, 0:1], rs[:, m:m + 1], ALU.subtract, ALU.mult).then_inc(nat_rdy, 1)
                for m in range(HC):
                    e.wait_ge(sg_rdy, 8 * i + (m + 1))
                    e.scalar_tensor_tensor(ha[:, m, :], pair[m % 2][:, 512:1024], sc2[:, m:m + 1], sg[:, m % 2, :], ALU.mult, ALU.mult).then_inc(gate_rdy, 1)
                e.wait_ge(o_t, i + 1)
                e.tensor_tensor(xt[:, :], pair[1][:, :], xt[:, :], ALU.add).then_inc(fin, 1)

    @block.tensor
    def _(e):
        with e.If(needed(e)):
            for n, base in NARROW:
                for u in range(2):
                    e.wait_ge(w_in[u], 8 * base + 16)
                    if base > 0:
                        e.wait_ge(w_ev, base + u - 1)
                    for c in range(HC):
                        ins = e.transpose(pair[u][:, c * P:(c + 1) * P], stage[u][:, c * P:(c + 1) * P], ident[:, :])
                    ins.then_inc(w_t, 1)
            for n, base in WIDE:
                with e.Fori(0, HC // 2) as k:
                    for q in range(2):
                        e.wait_ge(w_in[q], 16 * k + (8 * base + 16))
                        e.wait_ge(w_ev, 2 * k + (base + q - 1))
                        for c in range(HC):
                            ins = e.transpose(pair[q][:, c * P:(c + 1) * P], stage[q][:, c * P:(c + 1) * P], ident[:, :])
                        ins.then_inc(w_t, 1)
            e.wait_ge(w_ev, 6 + 2 * HC)

            def product(w, src, m, chunks, bank):
                for k in range(chunks):
                    ins = e.matmul(bank, w[:, k, m * P:(m + 1) * P], src(k), start=(k == 0), stop=(k == chunks - 1))
                return ins
            with e.Fori(0, NBLK) as i:
                e.wait_ge(nat_rdy, 4 * i + 4)
                for k in range(DH):
                    for m in range(TPB):
                        ins = e.transpose(pair[3][:, k * BLK + m * P:k * BLK + (m + 1) * P], nat[:, m, k * P:(k + 1) * P], ident[:, :])
                ins.then_inc(nat_t, 1)
                for m in range(HC):
                    if m == 0:
                        e.wait_ge(z_rdy, i + 1)
                        e.wait_ge(o_ev, 2 * i)
                    elif m == 1:
                        e.wait_ge(fin, i)
                    else:
                        e.wait_ge(gate_rdy, 8 * i + (m - 1))
                    for g, n in enumerate(("w1", "w2")):
                        ins = product(turned[n], lambda k: zT[:, k * BLK:(k + 1) * BLK], m, DH, pair[m % 2][:, 512 * g:512 * g + 512])
                    ins.then_inc(mm, 1)
                for s in range(2 * HC):
                    if s == 0:
                        e.wait_ge(gate_rdy, 8 * i + 8)
                    elif s == HC:
                        e.wait_ge(act_rdy, 16 * i + HC)
                    elif s >= 4:
                        e.wait_ge(act_rdy, 16 * i + (s - 3))
                    src = ha if s < HC else hb
                    product(turned["h1" if s < HC else "h2"], lambda k: src[:, k, :], s % HC, HC, h_ps[s % 4]).then_inc(mm, 1)
                for m in range(DH):
                    e.wait_ge(act_rdy, 16 * i + 2 * HC)
                    product(turned["w3"], lambda k: ha[:, k, :], m, HC, h_ps[m]).then_inc(mm, 1)
                e.wait_ge(o_ev, 2 * i + 2)
                for m in range(TPB):
                    for k in range(DH):
                        ins = e.transpose(pair[1][:, m * DM + k * P:m * DM + (k + 1) * P], sg[:, k, m * P:(m + 1) * P], ident[:, :])
                ins.then_inc(o_t, 1)


def decoder_layer(nc, a):
    with ExitStack() as ctx:
        t = {}
        t["ident"] = ctx.enter_context(nc.sbuf_tensor("ident", [P, P], F32))
        t["scl"] = ctx.enter_context(nc.sbuf_tensor("scl", [P, 4 * HC + DH], F32))
        t["pair"] = [ctx.enter_context(nc.psum_tensor(f"pair{k}", [P, 1024], F32)) for k in range(4)]
        t["flag"] = ctx.enter_context(nc.sbuf_tensor("flag", [1, 1], I32))
        kr_h = nc.dram_tensor("kernel_rows", [1, DM * L + L], F32, kind="Internal")
        al_h = nc.dram_tensor("alpha_rows", [DM, N], F32, kind="Internal")
        t["kr_h"], t["kr"], t["alS_h"], t["alS"] = kr_h, kr_h.ap(), al_h, al_h.ap()
        t["flag_col"] = nc.dram_tensor("flag_column", [P, 1], I32, kind="Internal").ap()
        t["x1d"] = nc.dram_tensor("x1_rows", [TOK, DM], F32, kind="Internal").ap()
        t["x2d"] = nc.dram_tensor("x2_rows", [TOK, DM], F32, kind="Internal").ap()
        with ExitStack() as shared:
            t["w1T"] = shared.enter_context(nc.sbuf_tensor("w1T", [P, DH, HID], F32R))
            t["h1T"] = shared.enter_context(nc.sbuf_tensor("h1T", [P, HC, HID], F32R))
            t["keysT"] = shared.enter_context(nc.sbuf_tensor("keysT", [P, BATCH * DH * KEYS], F32))
            t["x1t"] = shared.enter_context(nc.sbuf_tensor("x1t", [P, TPB * DM], F32))
            t["vb"] = shared.enter_context(nc.sbuf_tensor("vbuf", [P, 2, BLK], F32))
            t["sg"] = shared.enter_context(nc.sbuf_tensor("sg", [P, 2, BLK], F32))
            with ExitStack() as one:
                mixer_program(nc, one, a, t)
            with ExitStack() as two:
                attention_ffn_program(nc, two, a, t)
        with ExitStack() as three:
            exact_weights_program(nc, three, a, t)


_NAMES = {"x": "x", "ctx_1024": "ctx", "L0_attn_log_A": "logA", "L0_attn_B_param": "Bp", "L0_attn_C_param": "Cp",
          "L0_attn_D_param": "Dp", "L0_attn_log_dt": "log_dt", "L0_attn_ln_gamma": "gamma", "L0_attn_ln_beta": "beta",
          "L0_attn_W_out": "aW", "L0_attn_b_out": "ab", "L0_xattn_W_out": "xW", "L0_xattn_b_out": "xb",
          "L0_ffn_w1_w": "w1", "L0_ffn_w1_s": "s1", "L0_ffn_w2_w": "w2", "L0_ffn_w2_s": "s2", "L0_ffn_h1_w": "h1",
          "L0_ffn_h1_s": "hs1", "L0_ffn_h2_w": "h2", "L0_ffn_h2_s": "hs2", "L0_ffn_w3_w": "w3", "L0_ffn_w3_s": "s3"}


def kernel(**inputs):
    import concourse.bacc as _bacc
    from concourse.bass_utils import run_bass_kernel_spmd as _run

    nc = _bacc.Bacc("TRN2", target_bir_lowering=False, num_devices=1)
    arrays, aps = {}, {}
    for name, short in _NAMES.items():
        v = np.ascontiguousarray(inputs[name])
        arrays[f"in_{short}"] = v
        aps[short] = nc.dram_tensor(f"in_{short}", v.shape, mybir.dt.from_np(v.dtype), kind="ExternalInput").ap()
    aps["out"] = nc.dram_tensor("out", (BATCH, T, DM), F32, kind="ExternalOutput").ap()
    decoder_layer(nc, aps)
    r = _run(nc, [arrays], core_ids=[0])
    return r.results[0]["out"]
```
